# Optimizing a Trainium2 kernel written in Bass

```python
import numpy as np
import jax
import jax.numpy as jnp

def _softmax(x, axis=-1):
    return jax.nn.softmax(x, axis=axis)

def _gelu(x):
    return jax.nn.gelu(x, approximate=True)

def _silu(x):
    return jax.nn.silu(x)

def _sigmoid(x):
    return jax.nn.sigmoid(x)

def _layernorm(x, axis=-1, eps=1e-05):
    m = jnp.mean(x, axis=axis, keepdims=True)
    v = jnp.var(x, axis=axis, keepdims=True)
    return (x - m) / jnp.sqrt(v + eps)

def _scatter_add(tgt, idx, src, axis=0):
    return tgt.at[idx].add(src)

def _segment_sum(src, seg, n):
    return jax.ops.segment_sum(src, seg, n)
kernel_name = 'mk_adaln_d1_jaxref_r8_66064e'

def setup_inputs(seed: int=0):
    np.random.seed(seed)
    _w = jnp.asarray

    def _L0_attn_setup():
        import jax, jax.numpy as jnp
        import numpy as np
        H = 16

        def _split_heads(t):
            B, N, D = t.shape
            return t.reshape(B, N, H, D // H).transpose(0, 2, 1, 3)
        key = jax.random.key(seed)
        ks = jax.random.split(key, 9)
        B, N, D = (4, 512, 128)
        mk = lambda k, shape: jax.random.normal(k, shape, dtype=jnp.float32) * 0.02
        return {'x': jax.random.normal(ks[0], (B, N, D), dtype=jnp.float32), 'Wq': mk(ks[1], (D, D)), 'bq': mk(ks[2], (D,)), 'Wk': mk(ks[3], (D, D)), 'bk': mk(ks[4], (D,)), 'Wv': mk(ks[5], (D, D)), 'bv': mk(ks[6], (D,)), 'Wo': mk(ks[7], (D, D)), 'bo': mk(ks[8], (D,))}
    _L0_attn_in = _L0_attn_setup()

    def _L0_ffn_setup():
        import jax, jax.numpy as jnp
        import numpy as np
        D = 128
        E = 8
        K = 2
        DF = 512
        B, S = (2, 256)
        EPS_LN = 1e-05
        EPS_TOPK = 1e-08

        def _xavier(key, shape, fan_in, fan_out, dtype=jnp.float32):
            bound = float(np.sqrt(6.0 / (fan_in + fan_out)))
            return jax.random.uniform(key, shape, dtype, -bound, bound)
        key = jax.random.key(seed)
        kx, kg, k1, k2 = jax.random.split(key, 4)
        return {'x': jax.random.normal(kx, (B, S, D), jnp.float32), 'gamma': jnp.ones((D,), jnp.float32), 'beta': jnp.zeros((D,), jnp.float32), 'Wg': _xavier(kg, (E, D), D, E), 'bg': jnp.zeros((E,), jnp.float32), 'W1': _xavier(k1, (E, DF, D), D, DF), 'b1': jnp.zeros((E, DF), jnp.float32), 'W2': _xavier(k2, (E, D, DF), DF, D), 'b2': jnp.zeros((E, D), jnp.float32)}
    _L0_ffn_in = _L0_ffn_setup()
    _L0_c = _w((lambda *s: np.random.randn(*s).astype(np.float32) * 0.05)(8, 128))
    _L0_wmod = _w((lambda *s: np.random.randn(*s).astype(np.float32) * 0.05)(128, 6 * 128) * 128 ** (-0.5))
    _d = {'L0_attn_x': _L0_attn_in['x'], 'L0_attn_Wq': _L0_attn_in['Wq'], 'L0_attn_bq': _L0_attn_in['bq'], 'L0_attn_Wk': _L0_attn_in['Wk'], 'L0_attn_bk': _L0_attn_in['bk'], 'L0_attn_Wv': _L0_attn_in['Wv'], 'L0_attn_bv': _L0_attn_in['bv'], 'L0_attn_Wo': _L0_attn_in['Wo'], 'L0_attn_bo': _L0_attn_in['bo'], 'L0_ffn_gamma': _L0_ffn_in['gamma'], 'L0_ffn_beta': _L0_ffn_in['beta'], 'L0_ffn_Wg': _L0_ffn_in['Wg'], 'L0_ffn_bg': _L0_ffn_in['bg'], 'L0_ffn_W1': _L0_ffn_in['W1'], 'L0_ffn_b1': _L0_ffn_in['b1'], 'L0_ffn_W2': _L0_ffn_in['W2'], 'L0_ffn_b2': _L0_ffn_in['b2'], 'L0_c': _L0_c, 'L0_wmod': _L0_wmod}
    _x0 = _d['L0_attn_x']
    _d['L0_attn_x'] = jax.random.normal(jax.random.fold_in(jax.random.key(seed), 1), (8, 512, 128), dtype=_x0.dtype)
    del _x0
    return _d

def reference(L0_attn_x, L0_attn_Wq, L0_attn_bq, L0_attn_Wk, L0_attn_bk, L0_attn_Wv, L0_attn_bv, L0_attn_Wo, L0_attn_bo, L0_ffn_gamma, L0_ffn_beta, L0_ffn_Wg, L0_ffn_bg, L0_ffn_W1, L0_ffn_b1, L0_ffn_W2, L0_ffn_b2, L0_c, L0_wmod):

    def _L0_attn_ref(x, Wq, bq, Wk, bk, Wv, bv, Wo, bo):
        import jax, jax.numpy as jnp
        import numpy as np
        H = 16

        def _split_heads(t):
            B, N, D = t.shape
            return t.reshape(B, N, H, D // H).transpose(0, 2, 1, 3)
        B, N, D = x.shape
        d_head = D // H
        s = (d_head ** 0.5) ** (-0.25)
        q = _split_heads(x @ Wq + bq)
        _ = x @ Wk + bk
        v = _split_heads(x @ Wv + bv)
        q = jax.nn.softmax(q, axis=-1) * s
        k = jax.nn.softmax(q, axis=-2) * s
        ctx = jnp.einsum('bhnd,bhne->bhde', k, v)
        attn = jnp.einsum('bhnd,bhde->bhne', q, ctx)
        attn = attn.transpose(0, 2, 1, 3).reshape(B, N, D)
        return attn @ Wo + bo

    def _L0_ffn_ref(x, gamma, beta, Wg, bg, W1, b1, W2, b2):
        import jax, jax.numpy as jnp
        import numpy as np
        D = 128
        E = 8
        K = 2
        DF = 512
        B, S = (2, 256)
        EPS_LN = 1e-05
        EPS_TOPK = 1e-08

        def _xavier(key, shape, fan_in, fan_out, dtype=jnp.float32):
            bound = float(np.sqrt(6.0 / (fan_in + fan_out)))
            return jax.random.uniform(key, shape, dtype, -bound, bound)
        b, s, d = x.shape
        mu = jnp.mean(x, axis=-1, keepdims=True)
        var = jnp.mean((x - mu) ** 2, axis=-1, keepdims=True)
        xn = (x - mu) / jnp.sqrt(var + EPS_LN) * gamma + beta
        xf = xn.reshape(-1, d)
        logits = xf @ Wg.T + bg
        probs = jax.nn.softmax(logits, axis=-1)
        tp, ti = jax.lax.top_k(probs, K)
        tp = tp / (jnp.sum(tp, axis=-1, keepdims=True) + EPS_TOPK)
        w = jnp.sum(jax.nn.one_hot(ti, E, dtype=xf.dtype) * tp[..., None], axis=1)
        h = jax.nn.gelu(jnp.einsum('td,efd->tef', xf, W1) + b1, approximate=False)
        y = jnp.einsum('tef,edf->ted', h, W2) + b2
        out = jnp.einsum('ted,te->td', y, w)
        return x + out.reshape(b, s, d)
    x = L0_attn_x
    mod = (_silu(L0_c) @ L0_wmod).reshape(L0_c.shape[0], 6, 1, -1)
    sa, ca, ga, sb, cb, gb = (mod[:, 0], mod[:, 1], mod[:, 2], mod[:, 3], mod[:, 4], mod[:, 5])
    ga = (2 * (ga >= 0) - 1) * jnp.maximum(jnp.abs(ga), 0.25)
    gb = (2 * (gb >= 0) - 1) * jnp.maximum(jnp.abs(gb), 0.25)
    h = _layernorm(x, axis=-1) * (1 + ca) + sa
    x = x + ga * _L0_attn_ref(h, L0_attn_Wq, L0_attn_bq, L0_attn_Wk, L0_attn_bk, L0_attn_Wv, L0_attn_bv, L0_attn_Wo, L0_attn_bo)
    h = _layernorm(x, axis=-1) * (1 + cb) + sb
    x = x + gb * _L0_ffn_ref(h, L0_ffn_gamma, L0_ffn_beta, L0_ffn_Wg, L0_ffn_bg, L0_ffn_W1, L0_ffn_b1, L0_ffn_W2, L0_ffn_b2)
    return x

_drawn_inputs = setup_inputs


def setup_inputs(seed=0):
    import zlib

    import numpy as np

    out = dict(_drawn_inputs(seed))
    spreads = {'L0_ffn_gamma': (1.0, 0.2),
     'L0_ffn_beta': (0.0, 0.307),
     'L0_ffn_bg': (0.0, 0.529),
     'L0_ffn_b1': (0.0, 0.526),
     'L0_ffn_b2': (0.0, 0.432)}
    factors = {'L0_attn_Wq': 8.0,
     'L0_attn_bq': 8.0,
     'L0_attn_Wv': 8.0,
     'L0_attn_bv': 8.0,
     'L0_attn_Wo': 8.0,
     'L0_attn_bo': 8.0}
    for name, (base, spread) in spreads.items():
        noise = np.random.default_rng([zlib.crc32(name.encode()), seed]).standard_normal(out[name].shape)
        drawn = base * np.exp(spread * noise) if base else spread * noise
        out[name] = jnp.asarray(drawn.astype(out[name].dtype))
    for name, factor in factors.items():
        out[name] = (out[name] * factor).astype(out[name].dtype)
    return out
```

```python
from contextlib import ExitStack

import concourse.bass as bass
from concourse import mybir

F32 = mybir.dt.float32
F32R = mybir.dt.float32r
ACT = mybir.ActivationFunctionType
ALU = mybir.AluOpType
AX = mybir.AxisListType

P = 128
NB = 8
NJ = 4
TOK = P * NJ
G = 4
NG = NB // G
HEADS, DH = 16, 8
E = 8
CH = 4
NCH = E * CH
LAG = 3
RING = 4
EPS_LN = 1e-5
EPS_TOPK = 1e-8
GATE_STEPS = 20
S_QK = (DH ** 0.5) ** (-0.25)
ds = bass.ds


def adaln_block(nc, x, wq, wv, wo, bq, bv, bo, gamma, beta, wg, bg, w12, b1, b2, c_t, wmod, w_dram, out):
    with ExitStack() as ctx:
        def sb(name, shape, dt=F32):
            return ctx.enter_context(nc.sbuf_tensor(name, shape, dt))

        names = {}

        def sem(name):
            names[name] = ctx.enter_context(nc.semaphore(name))
            return names[name]

        X = sb("X", [P, NB * TOK])
        WH = sb("WH", [P, 2 * E * 512], F32R)
        WL = sb("WL", [P, 2 * E * 512], F32R)
        XH = sb("XH", [P, NB * TOK], F32R)
        XL = sb("XL", [P, NB * TOK], F32R)
        ROWS = sb("ROWS", [P, NB, 4, P])
        GABO = sb("GABO", [P, NB, P])
        HH = sb("HH", [P, RING, TOK], F32R)
        HL = sb("HL", [P, RING, TOK], F32R)
        STAGE = sb("STAGE", [P, 2, 512])
        WQV = sb("WQV", [P, 2, P])
        WO = sb("WO", [P, P])
        WG = sb("WG", [P, E])
        B1 = sb("B1", [P, NCH])
        B2 = sb("B2", [E, P])
        GB = sb("GB", [P, 2])
        BQV = sb("BQV", [1, 2, P])
        BG = sb("BG", [1, E])
        BO = sb("BO", [P, P])
        CT = sb("CT", [P, NB])
        SIL = sb("SIL", [P, 4, NB])
        MODT = sb("MODT", [P, 2, NB])
        IDENT = sb("IDENT", [P, P])
        HMASK = sb("HMASK", [P, HEADS, DH])
        ONES = sb("ONES", [P, P])
        NHALF = sb("NHALF", [P, G * NJ])
        RANK = sb("RANK", [P, G * NJ, E])
        ST = sb("ST", [P, 3, G * NJ, 6])
        MV = sb("MV", [P, 3, G * NJ, 2])
        VE = sb("VE", [P, 3, G * NJ])
        RSTD = sb("RSTD", [P, 3, G * NJ])
        SM = sb("SM", [P, G, 3, HEADS * NJ])
        CTX = sb("CTX", [P, G, P])
        RDEN = sb("RDEN", [P, G, 1])
        MS = sb("MS", [P, G, P])
        GS = sb("GS", [P, 8, G * NJ])
        ARENA = sb("ARENA", [P, 5 * G * TOK])

        def area(k):
            return ARENA[:, k * G * TOK:(k + 1) * G * TOK].rearrange("p (i n) -> p i n", i=G)

        XN, HT, V, EX, PR = (area(k) for k in range(5))
        GT = ARENA[:, G * TOK:G * TOK + 8 * G * NJ * E].rearrange("p (k a e) -> p k a e", k=8, e=E)
        WT = EX[0:E]
        WMOD = ARENA[:, 0:6 * P]
        SILB = ARENA[:, 1024:1024 + NB * P].rearrange("p (b n) -> p b n", b=NB)
        MAG = ARENA[:, 4096:4096 + NB * 4 * P].rearrange("p (b r n) -> p b r n", b=NB, r=4)
        HF = ARENA[:, 0:RING * TOK].rearrange("p (i n) -> p i n", i=RING)
        WB = ARENA[:, 2048:2048 + E * TOK].rearrange("p (e n) -> p e n", e=E)
        ACC = ARENA[:, 6144:6656]
        YW = ARENA[:, 6656:7168]
        YT = ARENA[:, 7168:7680]
        OT = ARENA[:, 7680:8192]

        bank = [ctx.enter_context(nc.psum_tensor(f"bank{k}", [P, 512], F32)) for k in range(8)]

        ld_x, ld_mod, ld_small, ld_w = sem("ld_x"), sem("ld_mod"), sem("ld_small"), [sem("ld_w0"), sem("ld_w1")]
        s_const, s_pc, s_es, s_sil, s_silb, s_modp, s_modt, s_rowp, s_rowc, s_rows, s_gabo, s_dset = (
            sem(n) for n in ("s_const", "s_pc", "s_es", "s_sil", "s_silb", "s_modp", "s_modt", "s_rowp", "s_rowc",
                             "s_rows", "s_gabo", "s_dset"))
        (s_st, s_mv, s_ve, s_rstd) = ([sem(f"{n}{k}") for k in range(3)] for n in ("s_st", "s_mv", "s_ve", "s_rstd"))
        (s_xn1, s_xg, s_xn1t, s_h1, s_q, s_v, s_mx, s_qs, s_vc, s_e, s_sm, s_rc, s_p, s_kx, s_pt, s_ptc, s_ctx, s_ct,
         s_m, s_ms, s_att, s_x1, s_xn2, s_t2, s_h2, s_xn3, s_xn3t, s_xf, s_xh, s_xl, s_lg, s_wt, s_wtc, s_b2w, s_h2b,
         s_r1, s_res) = (sem(n) for n in (
             "s_xn1", "s_xg", "s_xn1t", "s_h1", "s_q", "s_v", "s_mx", "s_qs", "s_vc", "s_e", "s_sm", "s_rc", "s_p",
             "s_kx", "s_pt", "s_ptc", "s_ctx", "s_ct", "s_m", "s_ms", "s_att", "s_x1", "s_xn2", "s_t2", "s_h2",
             "s_xn3", "s_xn3t", "s_xf", "s_xh", "s_xl", "s_lg", "s_wt", "s_wtc", "s_b2w", "s_h2b", "s_r1", "s_res"))
        s_gz, s_gez, s_gate, s_w = sem("s_gz"), sem("s_gez"), sem("s_gate"), sem("s_w")
        s_wh, s_wl = sem("s_wh"), sem("s_wl")
        st_w = sem("st_w")
        s_pre, s_gelu, s_hl, s_used, s_yread, s_acc, s_yt, s_ytt, s_o1, s_res2, st_out = (
            sem(n) for n in ("s_pre", "s_gelu", "s_hl", "s_used", "s_yread", "s_acc", "s_yt", "s_ytt", "s_o1",
                             "s_res2", "st_out"))
        ld_wb = [sem(f"ld_wb{e}") for e in range(E)]

        block = ctx.enter_context(nc.Block())

        x_p = x.rearrange("b (p j) d -> p b (j d)", j=NJ)
        out_p = out.rearrange("b (p j) d -> p b (j d)", j=NJ)
        heads = "p (m k) -> p m k"

        def tok(t, j):
            return t[:, j * P:(j + 1) * P]

        @block.sync
        def _(sp):
            sp.dma_start(CT[:], c_t).then_inc(ld_mod, 16)
            sp.dma_start(WMOD, wmod).then_inc(ld_mod, 16)
            sp.dma_start(X[:].rearrange("p (b n) -> p b n", b=NB), x_p).then_inc(ld_x, 16)
            for k in range(2 * E):
                if k >= 2:
                    sp.wait_ge(s_wl, k - 1)
                sp.dma_start(STAGE[:, k % 2, :], w12[:, k * 512:(k + 1) * 512]).then_inc(ld_w[k % 2], 16)
            sp.wait_ge(st_w, 16 * NB)
            sp.wait_ge(s_res, NB)
            sp.wait_ge(s_b2w, NB)
            sp.wait_ge(s_xl, NB)
            for e in range(E):
                sp.dma_start(WB[:, e, :], w_dram[0, e:e + 1, :].to_broadcast([P, TOK])).then_inc(ld_wb[e], 16)
            with sp.Fori(1, NB) as b:
                for e in range(E):
                    sp.wait_ge(s_yread, (b - 1) * E + e + 1)
                    sp.dma_start(WB[:, e, :], w_dram[ds(b, 1), e, :].to_broadcast([P, TOK])).then_inc(ld_wb[e], 16)
                    if e == 3:
                        sp.wait_ge(s_res2, b)
                        sp.dma_start(out_p[:, ds(b - 1, 1), :], X[:, ds((b - 1) * TOK, TOK)]).then_inc(st_out, 16)
            sp.wait_ge(s_res2, NB)
            sp.dma_start(out_p[:, NB - 1, :], X[:, (NB - 1) * TOK:NB * TOK]).then_inc(st_out, 16)
            sp.wait_ge(st_out, 16 * NB)

        @block.gpsimd
        def _(pool):
            pl = nc.gpsimd
            pl.memset(IDENT[:], 0.0).then_inc(s_pc, 1)
            pl.memset(HMASK[:], S_QK * S_QK).then_inc(s_pc, 1)
            pl.memset(NHALF[:], -0.5).then_inc(s_pc, 1)
            pl.memset(ONES[:], 1.0).then_inc(s_const, 1)
            pool.wait_ge(s_pc, 3)
            pl.affine_select(out=IDENT[:], in_=IDENT[:], compare_op=ALU.not_equal, fill=1.0, base=0,
                             pattern=[[-1, P]], channel_multiplier=1).then_inc(s_const, 1)
            pl.affine_select(out=HMASK[:], in_=HMASK[:], compare_op=ALU.is_ge, fill=0.0, base=0,
                             pattern=[[-DH, HEADS], [0, DH]], channel_multiplier=1).then_inc(s_pc, 1)
            pool.wait_ge(s_pc, 4)
            pl.affine_select(out=HMASK[:], in_=HMASK[:], compare_op=ALU.is_ge, fill=0.0, base=DH - 1,
                             pattern=[[DH, HEADS], [0, DH]], channel_multiplier=-1).then_inc(s_const, 1)
            pool.wait_ge(ld_small, 192)
            pool.wait_ge(s_rows, 1)
            pl.tensor_tensor(GABO[:], ROWS[:, :, 0, :], BO[:].unsqueeze(1).to_broadcast([P, NB, P]),
                             ALU.mult).then_inc(s_gabo, 1)
            pool.wait_ge(s_gabo, 1)

            def rstd(g, k, i):
                n = g * G + i + 1
                at = slice(i * NJ, (i + 1) * NJ)
                pool.wait_ge(s_mv[k], n)
                pl.tensor_scalar(VE[:, k, at], MV[:, k, at, 1], EPS_LN, None, ALU.add).then_inc(s_ve[k], 1)
                pool.wait_ge(s_ve[k], n)
                pl.tensor_tensor(RSTD[:, k, at], VE[:, k, at], NHALF[:, at], ALU.pow).then_inc(s_rstd[k], 1)

            for g in range(NG):
                for i in range(G):
                    rstd(g, 0, i)
                for i in range(G):
                    n = g * G + i + 1
                    xb = X[:, ds((g * G + i) * TOK, TOK)].rearrange("p (j d) -> p j d", j=NJ)
                    pool.wait_ge(s_xn1, n)
                    pl.tensor_tensor(xb, xb, GABO[:, ds(g * G + i, 1), :].to_broadcast([P, NJ, P]),
                                     ALU.add).then_inc(s_xg, 1)
                for i in range(G):
                    rstd(g, 1, i)
                for i in range(G):
                    n = g * G + i + 1
                    pool.wait_ge(s_xn2, n)
                    pl.tensor_tensor(V[:, i, :].rearrange("p (j d) -> p j d", j=NJ),
                                     XN[:, i, :].rearrange("p (j d) -> p j d", j=NJ),
                                     ROWS[:, ds(g * G + i, 1), 2, :].to_broadcast([P, NJ, P]),
                                     ALU.mult).then_inc(s_t2, 1)
                for i in range(G):
                    rstd(g, 2, i)
                for i in range(G):
                    n = g * G + i + 1
                    h2b = V[:, i, :].rearrange("p (j d) -> p j d", j=NJ)
                    pool.wait_ge(s_h2b, n)
                    pl.tensor_tensor(h2b, h2b, ROWS[:, ds(g * G + i, 1), 3, :].to_broadcast([P, NJ, P]),
                                     ALU.mult).then_inc(s_r1, 1)
                    xb = X[:, ds((g * G + i) * TOK, TOK)]
                    pool.wait_ge(s_r1, n)
                    pl.tensor_tensor(xb, xb, V[:, i, :], ALU.add).then_inc(s_res, 1)
                for k in range(E):
                    pool.wait_ge(s_wh, g * E + k + 1)
                    at = ds((g * E + k) * 512, 512)
                    pl.tensor_tensor(WL[:, at], STAGE[:, k % 2, :], WH[:, at].bitcast(F32),
                                     ALU.subtract).then_inc(s_wl, 1)

        @block.scalar
        def _(act):
            for dst, src in ((WQV[:, 0, :], wq), (WQV[:, 1, :], wv), (WO[:], wo), (WG[:], wg), (B1[:], b1),
                             (B2[:], b2), (GB[:, 0:1], gamma), (GB[:, 1:2], beta),
                             (BO[:], bo.to_broadcast([P, P]))):
                act.dma_start(dst, src).then_inc(ld_small, 16)
            for k, src in enumerate((bq, bv)):
                act.dma_start(BQV[:, k, :], src).then_inc(ld_small, 16)
            act.dma_start(BG[:], bg).then_inc(ld_small, 16)
            act.wait_ge(ld_mod, 32)
            nc.scalar.activation(SIL[:, 0, :], CT[:], ACT.Exp, scale=-1.0).then_inc(s_es, 1)
            for b in range(NB):
                act.wait_ge(s_rowp, b + 1)
                nc.scalar.activation(ROWS[:, b, :, :], bank[b][:].rearrange("p (r n) -> p r n", r=4),
                                     ACT.Copy).then_inc(s_rowc, 1)
            act.wait_ge(s_modt, 1)
            act.wait_ge(ld_small, 192)

            for g in range(NG):
                for i in range(G):
                    n = g * G + i + 1
                    act.wait_ge(s_xn1t, n)
                    nc.scalar.activation(HT[:, i, :], bank[i % 2][:], ACT.Identity,
                                         bias=MODT[:, 1, ds(g * G + i, 1)],
                                         scale=MODT[:, 0, ds(g * G + i, 1)]).then_inc(s_h1, 1)
                for i in range(G):
                    n = g * G + i + 1
                    act.wait_ge(s_v, n)
                    nc.scalar.activation(V[:, i, :], bank[4 + i % 2][:], ACT.Copy).then_inc(s_vc, 1)
                    act.wait_ge(s_qs, n)
                    nc.scalar.activation(EX[:, i, :], EX[:, i, :], ACT.Exp).then_inc(s_e, 1)
                for i in range(G):
                    n = g * G + i + 1
                    act.wait_ge(s_p, n)
                    nc.scalar.activation(EX[:, i, :], PR[:, i, :], ACT.Exp, scale=S_QK).then_inc(s_kx, 1)
                    act.wait_ge(s_pt, n)
                    nc.scalar.activation(HT[:, i, :], bank[6 + i % 2][:], ACT.Copy).then_inc(s_ptc, 1)
                for i in range(G):
                    n = g * G + i + 1
                    act.wait_ge(s_xn3t, n)
                    nc.scalar.activation(PR[:, i, :], bank[6 + i % 2][:], ACT.Identity,
                                         bias=GB[:, 1:2], scale=GB[:, 0:1]).then_inc(s_xf, 1)
                    act.wait_ge(s_xf, n)
                    nc.scalar.activation(XH[:, ds((g * G + i) * TOK, TOK)], PR[:, i, :],
                                         ACT.Copy).then_inc(s_xh, 1)
                act.wait_ge(s_gz, g + 1)
                nc.scalar.activation(GT[:, 1, :, :], GT[:, 0, :, :], ACT.Exp).then_inc(s_gez, 1)
                for i in range(G):
                    n = g * G + i + 1
                    act.wait_ge(s_wt, n)
                    nc.scalar.activation(WT[:, i, :], bank[2 + i][0:E, :], ACT.Copy).then_inc(s_wtc, 1)
                for i in range(G):
                    act.wait_ge(s_wtc, g * G + i + 1)
                    act.dma_start(w_dram[ds(g * G + i, 1)], WT[:, i, :]).then_inc(st_w, 16)
                for k in range(E):
                    act.wait_ge(ld_w[k % 2], (g * (E // 2) + k // 2 + 1) * 16)
                    nc.scalar.activation(WH[:, ds((g * E + k) * 512, 512)], STAGE[:, k % 2, :],
                                         ACT.Copy).then_inc(s_wh, 1)

            def gelus(b, first):
                for n in range(NCH):
                    slot = n % RING
                    done = b * NCH + n
                    act.wait_ge(s_pre, done + 1)
                    if not (first and n < RING):
                        act.wait_ge(s_used, done - RING + 1)
                    nc.scalar.activation(HF[:, slot, :], bank[slot][:], ACT.Gelu, bias=B1[:, n:n + 1])
                    nc.scalar.activation(HH[:, slot, :], bank[slot][:], ACT.Gelu,
                                         bias=B1[:, n:n + 1]).then_inc(s_gelu, 1)

            act.wait_ge(s_xl, NB)
            act.wait_ge(s_b2w, NB)
            act.wait_ge(s_res, NB)
            gelus(0, True)
            with act.Fori(1, NB) as b:
                gelus(b, False)

        @block.tensor
        def _(pe):
            mm = nc.tensor.matmul
            pe.wait_ge(ld_mod, 32)
            pe.wait_ge(s_sil, 1)
            for k, col in ((0, 1), (1, 0)):
                last = mm(bank[0][:, k * NB:(k + 1) * NB], WMOD[:, col * P:(col + 1) * P], SIL[:, 3, :],
                          start=True, stop=True)
            last.then_inc(s_modp, 1)
            pe.wait_ge(s_silb, 1)
            pe.wait_ge(s_modt, 1)
            for b in range(NB):
                mm(bank[b][:], SILB[:, b, :], WMOD[:, 2 * P:6 * P], start=True, stop=True).then_inc(s_rowp, 1)
            pe.wait_ge(s_const, 3)
            pe.wait_ge(ld_small, 192)
            pe.wait_ge(s_rowc, NB)

            def transposes(dst, src):
                for j in range(NJ):
                    last = nc.tensor.transpose(tok(dst, j), tok(src, j), IDENT[:])
                return last

            for g in range(NG):
                for i in range(G):
                    n = g * G + i + 1
                    pe.wait_ge(s_xn1, n)
                    if i >= 2:
                        pe.wait_ge(s_h1, n - 2)
                    transposes(bank[i % 2], XN[:, i, :]).then_inc(s_xn1t, 1)
                for i in range(G):
                    n = g * G + i + 1
                    pe.wait_ge(s_h1, n)
                    if i >= 2:
                        pe.wait_ge(s_qs, n - 2)
                        pe.wait_ge(s_vc, n - 2)
                    for k, done in ((0, s_q), (1, s_v)):
                        acc = bank[2 + 2 * k + i % 2]
                        mm(acc[:], ONES[0:1, :], BQV[:, k:k + 1, :].to_broadcast([1, NJ, P]),
                           start=True, stop=False, skip_group_check=True)
                        for j in range(NJ):
                            last = mm(tok(acc, j), tok(HT[:, i, :], j), WQV[:, k, :], start=False,
                                      stop=(j == NJ - 1), skip_group_check=True)
                        last.then_inc(done, 1)
                for i in range(G):
                    n = g * G + i + 1
                    pe.wait_ge(s_p, n)
                    if i >= 2:
                        pe.wait_ge(s_ptc, n - 2)
                    transposes(bank[6 + i % 2], PR[:, i, :]).then_inc(s_pt, 1)
                    pe.wait_ge(s_kx, n)
                    pe.wait_ge(s_vc, n)
                    if i >= 2:
                        pe.wait_ge(s_ct, n - 2)
                    ctx_ps = bank[i % 2]
                    for j in range(NJ):
                        mm(ctx_ps[:, 0:P], tok(V[:, i, :], j), tok(EX[:, i, :], j), start=(j == 0), stop=(j == NJ - 1))
                    for j in range(NJ):
                        last = mm(ctx_ps[:, P:P + 1], tok(EX[:, i, :], j), ONES[:, 0:1], start=(j == 0),
                                  stop=(j == NJ - 1))
                    last.then_inc(s_ctx, 1)
                for i in range(G):
                    n = g * G + i + 1
                    pe.wait_ge(s_ct, n)
                    if i >= 2:
                        pe.wait_ge(s_ms, n - 2)
                    mm(bank[2 + i % 2][:, 0:P], CTX[:, i, :], WO[:], start=True, stop=True).then_inc(s_m, 1)
                for i in range(G):
                    n = g * G + i + 1
                    pe.wait_ge(s_ms, n)
                    pe.wait_ge(s_ptc, n)
                    if i >= 2:
                        pe.wait_ge(s_x1, n - 2)
                    for j in range(NJ):
                        last = mm(tok(bank[4 + i % 2], j), tok(HT[:, i, :], j), MS[:, i, :], start=True, stop=True)
                    last.then_inc(s_att, 1)
                for i in range(G):
                    n = g * G + i + 1
                    pe.wait_ge(s_xn3, n)
                    if i >= 2:
                        pe.wait_ge(s_xf, n - 2)
                    transposes(bank[6 + i % 2], XN[:, i, :]).then_inc(s_xn3t, 1)
                mm(bank[0][:, 0:G * NJ * E], ONES[0:1, :], BG[:].unsqueeze(1).to_broadcast([1, G * NJ, E]), start=True, stop=False,
                   skip_group_check=True)
                for i in range(G):
                    pe.wait_ge(s_xf, g * G + i + 1)
                    for j in range(NJ):
                        at = (i * NJ + j) * E
                        last = mm(bank[0][:, at:at + E], tok(PR[:, i, :], j), WG[:], start=False,
                                  stop=(i * NJ + j == G * NJ - 1), skip_group_check=True)
                last.then_inc(s_lg, 1)
                pe.wait_ge(s_w, g + 1)
                for i in range(G):
                    for j in range(NJ):
                        last = nc.tensor.transpose(bank[2 + i][0:E, j * P:(j + 1) * P], GT[:, 7, i * NJ + j, :], IDENT[:])
                    last.then_inc(s_wt, 1)
                for i in range(G):
                    n = g * G + i + 1
                    pe.wait_ge(s_wtc, n)
                    if i >= 2:
                        pe.wait_ge(s_h2b, n - 2)
                    for j in range(NJ):
                        last = mm(tok(bank[i % 2], j), WT[:, i, j * P:(j + 1) * P], B2[:], start=True, stop=True)
                    last.then_inc(s_b2w, 1)

            pe.wait_ge(s_wl, 2 * E)
            pe.wait_ge(s_xl, NB)
            pe.wait_ge(s_h2b, NB)

            def first_product(b, n, first):
                done = b * NCH + n
                e, c = n // CH, n % CH
                if not (first and n < RING):
                    pe.wait_ge(s_gelu, done - RING + 1)
                w = slice(e * 1024 + c * P, e * 1024 + (c + 1) * P)
                xs = ds(b * TOK, TOK)
                mm(bank[n % RING][:], WH[:, w], XH[:, xs], start=True, stop=False)
                mm(bank[n % RING][:], WH[:, w], XL[:, xs], start=False, stop=False)
                mm(bank[n % RING][:], WL[:, w], XH[:, xs], start=False, stop=True).then_inc(s_pre, 1)

            def second_product(b, n, first):
                done = b * NCH + n
                e, c, slot = n // CH, n % CH, n % RING
                y = bank[4 + e % 2]
                if c == 0 and not (first and e < 2):
                    pe.wait_ge(s_yread, b * E + e - 1)
                w = slice(e * 1024 + 512 + c * P, e * 1024 + 512 + (c + 1) * P)
                pe.wait_ge(s_gelu, done + 1)
                mm(y[:], WH[:, w], HH[:, slot, :], start=(c == 0), stop=False)
                mm(y[:], WL[:, w], HH[:, slot, :], start=False, stop=False)
                pe.wait_ge(s_hl, done + 1)
                mm(y[:], WH[:, w], HL[:, slot, :], start=False, stop=(c == CH - 1)).then_inc(s_used, 1)

            def output_transposes(b):
                pe.wait_ge(s_yt, b + 1)
                transposes(bank[6], YT).then_inc(s_ytt, 1)

            def experts(b, first):
                for n in range(NCH):
                    first_product(b, n, first)
                    if n >= LAG:
                        second_product(b, n - LAG, first)
                    elif not first:
                        second_product(b - 1, n - LAG + NCH, False)
                    if n == 7 and not first:
                        output_transposes(b - 1)

            experts(0, True)
            with pe.Fori(1, NB) as b:
                experts(b, False)
            for n in range(NCH - LAG, NCH):
                second_product(NB - 1, n, False)
            output_transposes(NB - 1)

        @block.vector
        def _(dve):
            v = nc.vector
            for e in range(E):
                last = v.memset(RANK[:, :, e], float(E - e))
            last.then_inc(s_dset, 1)
            dve.wait_ge(s_es, 1)
            dve.wait_ge(ld_mod, 32)
            v.tensor_scalar(SIL[:, 1, :], SIL[:, 0, :], 1.0, None, ALU.add).then_inc(s_dset, 1)
            dve.wait_ge(s_dset, 2)
            v.reciprocal(SIL[:, 2, :], SIL[:, 1, :]).then_inc(s_dset, 1)
            dve.wait_ge(s_dset, 3)
            v.tensor_tensor(SIL[:, 3, :], CT[:], SIL[:, 2, :], ALU.mult).then_inc(s_sil, 1)
            dve.wait_ge(s_sil, 1)
            v.tensor_copy(SILB, SIL[:, 3, :].unsqueeze(2).to_broadcast([P, NB, P])).then_inc(s_silb, 1)
            dve.wait_ge(s_modp, 1)
            v.tensor_scalar(MODT[:, 0, :], bank[0][:, 0:NB], 1.0, None, ALU.add)
            v.tensor_copy(MODT[:, 1, :], bank[0][:, NB:2 * NB]).then_inc(s_modt, 1)
            dve.wait_ge(s_rowc, NB)
            v.scalar_tensor_tensor(out=MAG, in0=ROWS[:], scalar=-1.0, in1=ROWS[:], op0=ALU.mult,
                                   op1=ALU.max).then_inc(s_dset, 1)
            dve.wait_ge(s_dset, 4)
            v.tensor_scalar(MAG, MAG, 0.25, None, ALU.max).then_inc(s_dset, 1)
            for r in (0, 3):
                v.tensor_scalar(ROWS[:, :, r, :], ROWS[:, :, r, :], 0.0, 2.0, ALU.is_ge, ALU.mult).then_inc(s_dset, 1)
            v.tensor_scalar(ROWS[:, :, 2, :], ROWS[:, :, 2, :], 1.0, None, ALU.add).then_inc(s_dset, 1)
            dve.wait_ge(s_dset, 8)
            for r in (3, 0):
                last = v.scalar_tensor_tensor(out=ROWS[:, :, r, :], in0=ROWS[:, :, r, :], scalar=1.0,
                                              in1=MAG[:, :, r, :], op0=ALU.subtract, op1=ALU.mult)
            last.then_inc(s_rows, 1)
            dve.wait_ge(s_rows, 1)
            dve.wait_ge(ld_x, 16)

            def stats(g, k, i, src):
                n = g * G + i + 1
                for j in range(NJ):
                    last = v.bn_stats(ST[:, k, i * NJ + j, :], tok(src, j))
                last.then_inc(s_st[k], 1)
                dve.wait_ge(s_st[k], n)
                for j in range(NJ):
                    last = v.bn_aggr(MV[:, k, i * NJ + j, :], ST[:, k, i * NJ + j, :])
                last.then_inc(s_mv[k], 1)

            def normalise(g, k, i, src, done):
                dve.wait_ge(s_rstd[k], g * G + i + 1)
                for j in range(NJ):
                    a = i * NJ + j
                    last = v.tensor_scalar(tok(XN[:, i, :], j), tok(src, j), MV[:, k, a, 0:1], RSTD[:, k, a:a + 1],
                                           ALU.subtract, ALU.mult)
                last.then_inc(done, 1)

            for g in range(NG):
                def xb(i):
                    return X[:, ds((g * G + i) * TOK, TOK)]

                for i in range(G):
                    stats(g, 0, i, X[:, ds((g * G + i) * TOK, TOK)])
                for i in range(G):
                    normalise(g, 0, i, xb(i), s_xn1)
                for i in range(G):
                    n = g * G + i + 1
                    q = bank[2 + i % 2][:].rearrange(heads, k=DH)
                    dve.wait_ge(s_q, n)
                    v.tensor_reduce(SM[:, i, 0, :], q, AX.X, ALU.max).then_inc(s_mx, 1)
                    dve.wait_ge(s_mx, n)
                    v.tensor_tensor(EX[:, i, :].rearrange(heads, k=DH), q,
                                    SM[:, i, 0, :].unsqueeze(2).to_broadcast([P, HEADS * NJ, DH]),
                                    ALU.subtract).then_inc(s_qs, 1)
                for i in range(G):
                    n = g * G + i + 1
                    ex = EX[:, i, :].rearrange(heads, k=DH)
                    dve.wait_ge(s_e, n)
                    v.tensor_reduce(SM[:, i, 1, :], ex, AX.X, ALU.add).then_inc(s_sm, 1)
                    dve.wait_ge(s_sm, n)
                    v.reciprocal(SM[:, i, 2, :], SM[:, i, 1, :]).then_inc(s_rc, 1)
                    dve.wait_ge(s_rc, n)
                    v.tensor_tensor(PR[:, i, :].rearrange(heads, k=DH), ex,
                                    SM[:, i, 2, :].unsqueeze(2).to_broadcast([P, HEADS * NJ, DH]),
                                    ALU.mult).then_inc(s_p, 1)
                for i in range(G):
                    dve.wait_ge(s_ctx, g * G + i + 1)
                    v.tensor_tensor(CTX[:, i, :], bank[i % 2][:, 0:P], HMASK[:].rearrange("p m k -> p (m k)"),
                                    ALU.mult)
                    v.reciprocal(RDEN[:, i, :], bank[i % 2][:, P:P + 1]).then_inc(s_ct, 1)
                for i in range(G):
                    dve.wait_ge(s_m, g * G + i + 1)
                    v.scalar_tensor_tensor(out=MS[:, i, :], in0=bank[2 + i % 2][:, 0:P], scalar=RDEN[:, i, 0:1],
                                           in1=ROWS[:, ds(g * G + i, 1), 0, :].rearrange("p b n -> p (b n)"),
                                           op0=ALU.mult, op1=ALU.mult).then_inc(s_ms, 1)
                for i in range(G):
                    n = g * G + i + 1
                    dve.wait_ge(s_att, n)
                    dve.wait_ge(s_xg, n)
                    v.tensor_tensor(xb(i), bank[4 + i % 2][:], xb(i), ALU.add).then_inc(s_x1, 1)
                    dve.wait_ge(s_x1, n)
                    stats(g, 1, i, xb(i))
                for i in range(G):
                    normalise(g, 1, i, xb(i), s_xn2)
                for i in range(G):
                    n = g * G + i + 1
                    h2 = V[:, i, :].rearrange("p (j d) -> p j d", j=NJ)
                    dve.wait_ge(s_t2, n)
                    v.tensor_tensor(h2, h2, ROWS[:, ds(g * G + i, 1), 1, :].to_broadcast([P, NJ, P]),
                                    ALU.add).then_inc(s_h2, 1)
                    dve.wait_ge(s_h2, n)
                    stats(g, 2, i, V[:, i, :])
                for i in range(G):
                    normalise(g, 2, i, V[:, i, :], s_xn3)
                for i in range(G):
                    n = g * G + i + 1
                    at = ds((g * G + i) * TOK, TOK)
                    dve.wait_ge(s_xh, n)
                    v.tensor_tensor(XL[:, at], PR[:, i, :], XH[:, at].bitcast(F32), ALU.subtract).then_inc(s_xl, 1)
                z, ez, pr, eq, first_hot, rest, second_hot, w = (GT[:, k, :, :] for k in range(8))
                top, total, inv, best, rank1, second, rank2, scale = (GS[:, k, :] for k in range(8))

                def wide(t):
                    return t.unsqueeze(2).to_broadcast([P, G * NJ, E])

                steps = [0]

                def link(ins):
                    steps[0] += 1
                    ins.then_inc(s_gate, 1)
                    dve.wait_ge(s_gate, g * GATE_STEPS + steps[0])

                logits = bank[0][:, 0:G * NJ * E].rearrange("p (a e) -> p a e", e=E)
                dve.wait_ge(s_lg, g + 1)
                link(v.tensor_reduce(top, logits, AX.X, ALU.max))
                v.tensor_tensor(z, logits, wide(top), ALU.subtract).then_inc(s_gz, 1)
                dve.wait_ge(s_gez, g + 1)
                link(v.tensor_reduce(total, ez, AX.X, ALU.add))
                link(v.reciprocal(inv, total))
                link(v.tensor_tensor(pr, ez, wide(inv), ALU.mult))
                link(v.tensor_reduce(best, pr, AX.X, ALU.max))
                link(v.tensor_tensor(eq, pr, wide(best), ALU.is_equal))
                link(v.tensor_tensor(eq, eq, RANK[:], ALU.mult))
                link(v.tensor_reduce(rank1, eq, AX.X, ALU.max))
                link(v.tensor_tensor(first_hot, eq, wide(rank1), ALU.is_equal))
                link(v.scalar_tensor_tensor(out=rest, in0=first_hot, scalar=-2.0, in1=pr, op0=ALU.mult, op1=ALU.add))
                link(v.tensor_reduce(second, rest, AX.X, ALU.max))
                link(v.tensor_tensor(eq, rest, wide(second), ALU.is_equal))
                link(v.tensor_tensor(eq, eq, RANK[:], ALU.mult))
                link(v.tensor_reduce(rank2, eq, AX.X, ALU.max))
                link(v.tensor_tensor(second_hot, eq, wide(rank2), ALU.is_equal))
                link(v.tensor_tensor(first_hot, first_hot, second_hot, ALU.add))
                link(v.tensor_tensor(scale, best, second, ALU.add))
                link(v.tensor_scalar(scale, scale, EPS_TOPK, None, ALU.add))
                link(v.reciprocal(scale, scale))
                link(v.tensor_tensor(w, pr, first_hot, ALU.mult))
                assert steps[0] == GATE_STEPS
                v.tensor_tensor(w, w, wide(scale), ALU.mult).then_inc(s_w, 1)
                for i in range(G):
                    n = g * G + i + 1
                    dve.wait_ge(s_b2w, n)
                    v.tensor_tensor(V[:, i, :], bank[i % 2][:], V[:, i, :], ALU.add).then_inc(s_h2b, 1)
                dve.wait_ge(st_w, (g + 1) * G * 16)

            def lo(b, n, first):
                slot = n % RING
                done = b * NCH + n
                dve.wait_ge(s_gelu, done + 1)
                if not (first and n < RING):
                    dve.wait_ge(s_used, done - RING + 1)
                v.tensor_tensor(HL[:, slot, :], HF[:, slot, :], HH[:, slot, :].bitcast(F32),
                                ALU.subtract).then_inc(s_hl, 1)

            def gated(b, e):
                done = b * E + e
                dve.wait_ge(s_used, done * CH + CH)
                dve.wait_ge(ld_wb[e], (b + 1) * 16)
                y = bank[4 + e % 2][:]
                if e == 0:
                    v.tensor_tensor(ACC, y, WB[:, e, :], ALU.mult).then_inc(s_yread, 1)
                    return
                v.tensor_tensor(YW, y, WB[:, e, :], ALU.mult).then_inc(s_yread, 1)
                dve.wait_ge(s_yread, done + 1)
                if e > 1:
                    dve.wait_ge(s_acc, b * (E - 2) + e - 1)
                if e < E - 1:
                    v.tensor_tensor(ACC, ACC, YW, ALU.add).then_inc(s_acc, 1)
                else:
                    v.tensor_tensor(YT, ACC, YW, ALU.add).then_inc(s_yt, 1)

            def result(b):
                dve.wait_ge(s_ytt, b + 1)
                v.tensor_tensor(OT.rearrange("p (j d) -> p j d", j=NJ), bank[6][:].rearrange("p (j d) -> p j d", j=NJ),
                                ROWS[:, ds(b, 1), 3, :].to_broadcast([P, NJ, P]), ALU.mult).then_inc(s_o1, 1)
                dve.wait_ge(s_o1, b + 1)
                xr = X[:, ds(b * TOK, TOK)]
                v.tensor_tensor(xr, xr, OT, ALU.add).then_inc(s_res2, 1)

            def experts(b, first):
                for n in range(NCH):
                    lo(b, n, first)
                    if n % CH == 1 and n > CH:
                        gated(b, n // CH - 1)
                    if n == 1 and not first:
                        gated(b - 1, E - 1)
                    if n == 11 and not first:
                        result(b - 1)

            dve.wait_ge(s_res, NB)
            experts(0, True)
            with dve.Fori(1, NB) as b:
                experts(b, False)
            gated(NB - 1, E - 1)
            result(NB - 1)


def kernel(**inputs):
    import numpy as _np
    import concourse.bacc as _bacc
    from concourse.bass_utils import run_bass_kernel_spmd as _run

    a = {k: _np.asarray(v) for k, v in inputs.items()}
    d, e, f = P, E, CH * P
    w1 = a["L0_ffn_W1"].transpose(2, 0, 1)
    w2 = a["L0_ffn_W2"].transpose(0, 2, 1).reshape(e, CH, P, d).transpose(2, 0, 1, 3).reshape(P, e, CH * d)
    arrays = {
        "x": a["L0_attn_x"],
        "wq": a["L0_attn_Wq"], "wv": a["L0_attn_Wv"], "wo": a["L0_attn_Wo"],
        "bq": a["L0_attn_bq"].reshape(1, d), "bv": a["L0_attn_bv"].reshape(1, d), "bo": a["L0_attn_bo"].reshape(1, d),
        "gamma": a["L0_ffn_gamma"].reshape(d, 1), "beta": a["L0_ffn_beta"].reshape(d, 1),
        "wg": a["L0_ffn_Wg"].T, "bg": a["L0_ffn_bg"].reshape(1, e),
        "w12": _np.stack([w1, w2], axis=2).reshape(P, 2 * e * f),
        "b1": a["L0_ffn_b1"].reshape(e * CH, P).T, "b2": a["L0_ffn_b2"],
        "c_t": a["L0_c"].T, "wmod": a["L0_wmod"],
    }
    arrays = {k: _np.ascontiguousarray(v) for k, v in arrays.items()}
    nc = _bacc.Bacc("TRN2", target_bir_lowering=False, num_devices=1)
    args = {k: nc.dram_tensor(k, v.shape, F32, kind="ExternalInput").ap() for k, v in arrays.items()}
    w_dram = nc.dram_tensor("w_dram", (NB, E, TOK), F32).ap()
    out = nc.dram_tensor("out", (NB, TOK, P), F32, kind="ExternalOutput").ap()
    adaln_block(nc, w_dram=w_dram, out=out, **args)
    r = _run(nc, [arrays], core_ids=[0])
    return r.results[0]["out"]
```

```python
from contextlib import ExitStack

import concourse.bass as bass
from concourse import mybir

F32 = mybir.dt.float32
F32R = mybir.dt.float32r
ACT = mybir.ActivationFunctionType
ALU = mybir.AluOpType
AX = mybir.AxisListType

P = 128
NB = 8
NJ = 4
TOK = P * NJ
G = 4
NG = NB // G
HEADS, DH = 16, 8
E = 8
CH = 4
NCH = E * CH
LAG = 3
RING = 4
EPS_LN = 1e-5
EPS_TOPK = 1e-8
S_QK = (DH ** 0.5) ** (-0.25)
ds = bass.ds


def adaln_block(nc, x, wqv, wo, bqv, bo, gb, wg, bg, w12, b1, b2, c_t, wmod, mod_dram, w_dram, out):
    with ExitStack() as ctx:
        def sb(name, shape, dt=F32):
            return ctx.enter_context(nc.sbuf_tensor(name, shape, dt))

        names = {}

        def sem(name):
            names[name] = ctx.enter_context(nc.semaphore(name))
            return names[name]

        X = sb("X", [P, NB * TOK])
        WH = sb("WH", [P, 2 * E * 512], F32R)
        WL = sb("WL", [P, 2 * E * 512], F32R)
        XH = sb("XH", [P, NB * TOK], F32R)
        XL = sb("XL", [P, NB * TOK], F32R)
        ROWS = sb("ROWS", [P, NB, 5, P])
        HH = sb("HH", [P, RING, TOK], F32R)
        HL = sb("HL", [P, RING, TOK], F32R)
        STAGE = sb("STAGE", [P, 2, 512])
        WQV = sb("WQV", [P, 2, P])
        WO = sb("WO", [P, P])
        WG = sb("WG", [P, E])
        B1 = sb("B1", [P, NCH])
        B2 = sb("B2", [P, E])
        GB = sb("GB", [P, 2])
        BQV = sb("BQV", [64, 2, P], F32R)
        ONESR = sb("ONESR", [P, P], F32R)
        BG = sb("BG", [1, E])
        CT = sb("CT", [P, NB])
        SIL = sb("SIL", [P, 4, NB])
        MODT = sb("MODT", [P, 2, NB])
        IDENT = sb("IDENT", [P, P])
        HMASK = sb("HMASK", [P, HEADS, DH])
        NHALF = sb("NHALF", [P, NJ])
        RANK = sb("RANK", [P, E])
        ST = sb("ST", [P, 3, NB * NJ, 6])
        MV = sb("MV", [P, 3, NB * NJ, 2])
        VE = sb("VE", [P, 3, NB * NJ])
        RSTD = sb("RSTD", [P, 3, NB * NJ])
        NMR = sb("NMR", [P, 3, NB * NJ])
        SM = sb("SM", [P, 2, 3, HEADS * NJ])
        CTX = sb("CTX", [P, G, P])
        RDEN = sb("RDEN", [P, G, 1])
        MS = CTX
        GT = sb("GT", [P, 5, G * NJ, E])
        GS = sb("GS", [P, 8, G * NJ])
        WT = sb("WT", [P, P])
        ARENA = sb("ARENA", [P, 5 * G * TOK])

        def area(k):
            return ARENA[:, k * G * TOK:(k + 1) * G * TOK].rearrange("p (i n) -> p i n", i=G)

        XN, HT, V, EX, PR = (area(k) for k in range(5))
        WMOD = ARENA[:, 4 * G * TOK:4 * G * TOK + 6 * P]
        MOD8 = ARENA[0:NB, 4 * G * TOK + 6 * P:4 * G * TOK + 11 * P].rearrange("p (r n) -> p r n", r=5)
        MAG8 = ARENA[0:NB, 3 * G * TOK:3 * G * TOK + 6 * P].rearrange("p (k r n) -> p k r n", k=3, r=2)
        BRAW = ARENA[0:64, 3 * G * TOK + 6 * P:3 * G * TOK + 8 * P].rearrange("p (k n) -> p k n", k=2)
        BO = ARENA[0:NB, 3 * G * TOK + 8 * P:3 * G * TOK + 9 * P]
        ONES = ARENA[:, 3 * G * TOK + 9 * P:3 * G * TOK + 10 * P]
        HF = XN
        ACC, YW, YT, OT = (HT[:, k, :] for k in range(4))
        WB = ARENA[:, 3 * G * TOK:3 * G * TOK + E * TOK].rearrange("p (e n) -> p e n", e=E)

        bank = [ctx.enter_context(nc.psum_tensor(f"bank{k}", [P, 512], F32)) for k in range(8)]

        ld_x = [sem(f"ld_x{b}") for b in range(NB)]
        ld_mod, ld_qv, ld_small, ld_rows = sem("ld_mod"), sem("ld_qv"), sem("ld_small"), sem("ld_rows")
        ld_w = [sem("ld_w0"), sem("ld_w1")]
        s_const, s_pc, s_zero, s_es, s_sil, s_bqv, s_modp, s_modt, s_mod8p, s_mod8, s_dset, st_mod = (
            sem(n) for n in ("s_const", "s_pc", "s_zero", "s_es", "s_sil", "s_bqv", "s_modp", "s_modt", "s_mod8p",
                             "s_mod8", "s_dset", "st_mod"))
        (s_st, s_mv, s_ve, s_rstd) = ([sem(f"{n}{k}") for k in range(3)] for n in ("s_st", "s_mv", "s_ve", "s_rstd"))
        s_nmr = {k: sem(f"s_nmr{k}") for k in (0, 2)}
        (s_xn1, s_xg, s_xn1t, s_h1, s_q, s_v, s_mx, s_qs, s_vc, s_e, s_sm, s_rc, s_p, s_kx, s_pt, s_ptc, s_ctx, s_ct,
         s_m, s_ms, s_att, s_x1, s_xn2, s_t2, s_h2, s_xn3, s_xn3t, s_xf, s_xh, s_xl, s_lg, s_wt, s_wtc,
         s_r1, s_res) = (sem(n) for n in (
             "s_xn1", "s_xg", "s_xn1t", "s_h1", "s_q", "s_v", "s_mx", "s_qs", "s_vc", "s_e", "s_sm", "s_rc", "s_p",
             "s_kx", "s_pt", "s_ptc", "s_ctx", "s_ct", "s_m", "s_ms", "s_att", "s_x1", "s_xn2", "s_t2", "s_h2",
             "s_xn3", "s_xn3t", "s_xf", "s_xh", "s_xl", "s_lg", "s_wt", "s_wtc", "s_r1", "s_res"))
        s_gz, s_gez, s_gate, s_w = sem("s_gz"), sem("s_gez"), sem("s_gate"), sem("s_w")
        s_wh, s_wl = sem("s_wh"), sem("s_wl")
        st_w = [sem("st_w0"), sem("st_w1")]
        s_pre, s_gelu, s_hl, s_used, s_yread, s_acc, s_yt, s_ytt, s_o1, s_res2, st_out = (
            sem(n) for n in ("s_pre", "s_gelu", "s_hl", "s_used", "s_yread", "s_acc", "s_yt", "s_ytt", "s_o1",
                             "s_res2", "st_out"))
        ld_wb = [sem(f"ld_wb{e}") for e in range(E)]

        block = ctx.enter_context(nc.Block())

        x_p = x.rearrange("b (p j) d -> p b (j d)", j=NJ)
        out_p = out.rearrange("b (p j) d -> p b (j d)", j=NJ)
        heads = "p (m k) -> p m k"

        def tok(t, j):
            return t[:, j * P:(j + 1) * P]

        def per_token(t):
            return t.rearrange("p (j d) -> p j d", j=NJ)

        def logits_ps(g):
            return bank[7][:, 2 * g * P:(2 * g + 1) * P]

        def gates_ps(g):
            return bank[7][:, (2 * g + 1) * P:(2 * g + 2) * P]

        @block.sync
        def _(sp):
            sp.dma_start(CT[:], c_t).then_inc(ld_mod, 16)
            sp.dma_start(WMOD, wmod).then_inc(ld_mod, 16)
            for b in range(NB):
                sp.dma_start(X[:, b * TOK:(b + 1) * TOK], x_p[:, b, :]).then_inc(ld_x[b], 16)
            for k in range(2 * E):
                if k >= 2:
                    sp.wait_ge(s_wl, k - 1)
                sp.dma_start(STAGE[:, k % 2, :], w12[:, k * 512:(k + 1) * 512]).then_inc(ld_w[k % 2], 16)
                if k == 1:
                    sp.wait_ge(s_mod8, 1)
                    sp.dma_start(mod_dram, MOD8[:]).then_inc(st_mod, 16)
                    sp.wait_ge(st_mod, 16)
                    sp.dma_start(ROWS[:], mod_dram.unsqueeze(0).to_broadcast([P, NB, 5, P])).then_inc(ld_rows, 16)
            sp.wait_ge(s_lg, NG)
            sp.wait_ge(s_xl, NB)
            sp.wait_ge(st_w[0], 16)
            for e in range(E):
                sp.dma_start(per_token(WB[:, e, :]), w_dram[0:1, :, e, :].to_broadcast([P, NJ, P])).then_inc(ld_wb[e], 16)
            sp.wait_ge(st_w[1], 16)
            with sp.Fori(1, NB) as b:
                for e in range(E):
                    sp.wait_ge(s_yread, (b - 1) * E + e + 1)
                    sp.dma_start(per_token(WB[:, e, :]),
                                 w_dram[ds(b, 1), :, e, :].to_broadcast([P, NJ, P])).then_inc(ld_wb[e], 16)
                    if e == 3:
                        sp.wait_ge(s_res2, b)
                        sp.dma_start(out_p[:, ds(b - 1, 1), :], X[:, ds((b - 1) * TOK, TOK)]).then_inc(st_out, 16)
            sp.wait_ge(s_res2, NB)
            sp.dma_start(out_p[:, NB - 1, :], X[:, (NB - 1) * TOK:NB * TOK]).then_inc(st_out, 16)
            sp.wait_ge(st_out, 16 * NB)

        @block.gpsimd
        def _(pool):
            pl = nc.gpsimd
            pl.memset(IDENT[:], 0.0).then_inc(s_pc, 1)
            pl.memset(HMASK[:], S_QK * S_QK).then_inc(s_pc, 1)
            pl.memset(NHALF[:], -0.5).then_inc(s_pc, 1)
            pl.memset(ONES[:], 1.0).then_inc(s_const, 1)
            pool.wait_ge(s_pc, 3)
            pl.affine_select(out=IDENT[:], in_=IDENT[:], compare_op=ALU.not_equal, fill=1.0, base=0,
                             pattern=[[-1, P]], channel_multiplier=1).then_inc(s_const, 1)
            pl.affine_select(out=HMASK[:], in_=HMASK[:], compare_op=ALU.is_ge, fill=0.0, base=0,
                             pattern=[[-DH, HEADS], [0, DH]], channel_multiplier=1).then_inc(s_pc, 1)
            pool.wait_ge(s_pc, 4)
            pl.affine_select(out=HMASK[:], in_=HMASK[:], compare_op=ALU.is_ge, fill=0.0, base=DH - 1,
                             pattern=[[DH, HEADS], [0, DH]], channel_multiplier=-1).then_inc(s_const, 1)

            def rstd(k, b):
                at = slice(b * NJ, (b + 1) * NJ)
                pool.wait_ge(s_mv[k], b + 1)
                pl.tensor_scalar(VE[:, k, at], MV[:, k, at, 1], EPS_LN, None, ALU.add).then_inc(s_ve[k], 1)
                pool.wait_ge(s_ve[k], b + 1)
                pl.tensor_tensor(RSTD[:, k, at], VE[:, k, at], NHALF[:], ALU.pow).then_inc(s_rstd[k], 1)

            def weight_lo(k):
                pool.wait_ge(s_wh, k + 1)
                at = slice(k * 512, (k + 1) * 512)
                pl.tensor_tensor(WL[:, at], STAGE[:, k % 2, :], WH[:, at].bitcast(F32), ALU.subtract).then_inc(s_wl, 1)

            def residual(g):
                for i in range(G):
                    b = g * G + i
                    h2 = per_token(V[:, i, :])
                    pool.wait_ge(s_xn3, b + 1)
                    pl.tensor_tensor(h2, h2, ROWS[:, b:b + 1, 3, :].to_broadcast([P, NJ, P]), ALU.mult).then_inc(s_r1, 1)
                    xb = X[:, b * TOK:(b + 1) * TOK]
                    pool.wait_ge(s_r1, b + 1)
                    pl.tensor_tensor(xb, xb, V[:, i, :], ALU.add).then_inc(s_res, 1)

            for b in range(NB):
                rstd(0, b)
            pool.wait_ge(ld_rows, 16)
            for g in range(NG):
                if g > 0:
                    residual(g - 1)
                for i in range(G):
                    b = g * G + i
                    xb = per_token(X[:, b * TOK:(b + 1) * TOK])
                    pool.wait_ge(s_xn1, b + 1)
                    pl.tensor_tensor(xb, xb, ROWS[:, b:b + 1, 4, :].to_broadcast([P, NJ, P]), ALU.add).then_inc(s_xg, 1)
                for k in range(g * E, g * E + 4):
                    weight_lo(k)
                for i in range(G):
                    rstd(1, g * G + i)
                for i in range(G):
                    b = g * G + i
                    pool.wait_ge(s_xn2, b + 1)
                    pl.tensor_tensor(per_token(V[:, i, :]), per_token(XN[:, i, :]),
                                     ROWS[:, b:b + 1, 2, :].to_broadcast([P, NJ, P]), ALU.mult).then_inc(s_t2, 1)
                for i in range(G):
                    rstd(2, g * G + i)
                for k in range(g * E + 4, (g + 1) * E):
                    weight_lo(k)
            residual(NG - 1)

        @block.scalar
        def _(act):
            act.dma_start(WQV[:], wqv).then_inc(ld_qv, 16)
            act.wait_ge(s_zero, 1)
            for part in (0, 32):
                act.dma_start(BRAW[part:part + 1, :, :], bqv).then_inc(ld_qv, 16)
            act.wait_ge(ld_mod, 32)
            nc.scalar.activation(SIL[:, 0, :], CT[:], ACT.Exp, scale=-1.0).then_inc(s_es, 1)
            for dst, src in ((WO[:], wo), (WG[:], wg), (B1[:], b1), (B2[:], b2), (GB[:], gb),
                             (BO[:], bo.to_broadcast([NB, P])), (BG[:], bg)):
                act.dma_start(dst, src).then_inc(ld_small, 16)

            def norm(k, b, src, done):
                act.wait_ge(s_nmr[k], b + 1)
                for j in range(NJ):
                    a = b * NJ + j
                    last = nc.scalar.activation(tok(XN[:, b % G, :], j), tok(src, j), ACT.Identity,
                                                bias=NMR[:, k, a:a + 1], scale=RSTD[:, k, a:a + 1])
                last.then_inc(done, 1)

            def weight_hi(k):
                act.wait_ge(ld_w[k % 2], (k // 2 + 1) * 16)
                nc.scalar.activation(WH[:, k * 512:(k + 1) * 512], STAGE[:, k % 2, :], ACT.Copy).then_inc(s_wh, 1)

            def gates_store(g):
                act.wait_ge(s_wt, g + 1)
                if g > 0:
                    act.wait_ge(st_w[g - 1], 16)
                nc.scalar.activation(WT[:], gates_ps(g), ACT.Copy).then_inc(s_wtc, 1)
                act.wait_ge(s_wtc, g + 1)
                act.dma_start(w_dram[g * G:(g + 1) * G].rearrange("b j e p -> (b j e) p"), WT[:]).then_inc(st_w[g], 16)

            for g in range(NG):
                for i in range(G):
                    b = g * G + i
                    norm(0, b, X[:, b * TOK:(b + 1) * TOK], s_xn1)
                if g == 0:
                    act.wait_ge(s_modt, 1)
                    act.wait_ge(ld_small, 112)
                for i in range(G):
                    b = g * G + i
                    act.wait_ge(s_xn1t, b + 1)
                    nc.scalar.activation(HT[:, i, :], bank[i % 2][:], ACT.Identity, bias=MODT[:, 1, b:b + 1],
                                         scale=MODT[:, 0, b:b + 1]).then_inc(s_h1, 1)
                for k in (0, 1):
                    weight_hi(g * E + k)
                for i in range(G):
                    n = g * G + i + 1
                    act.wait_ge(s_v, n)
                    if g > 0:
                        act.wait_ge(s_res, n - G)
                    nc.scalar.activation(V[:, i, :], bank[4 + i % 2][:], ACT.Copy).then_inc(s_vc, 1)
                    act.wait_ge(s_qs, n)
                    nc.scalar.activation(EX[:, i, :], EX[:, i, :], ACT.Exp).then_inc(s_e, 1)
                if g > 0:
                    gates_store(g - 1)
                for i in range(G):
                    n = g * G + i + 1
                    act.wait_ge(s_p, n)
                    nc.scalar.activation(EX[:, i, :], PR[:, i, :], ACT.Exp, scale=S_QK).then_inc(s_kx, 1)
                    act.wait_ge(s_pt, n)
                    nc.scalar.activation(HT[:, i, :], bank[2 + i % 2][:], ACT.Copy).then_inc(s_ptc, 1)
                for k in (2, 3):
                    weight_hi(g * E + k)
                for i in range(G):
                    norm(2, g * G + i, V[:, i, :], s_xn3)
                for i in range(G):
                    b = g * G + i
                    act.wait_ge(s_xn3t, b + 1)
                    nc.scalar.activation(PR[:, i, :], bank[i % 2][:], ACT.Identity,
                                         bias=GB[:, 1:2], scale=GB[:, 0:1]).then_inc(s_xf, 1)
                    act.wait_ge(s_xf, b + 1)
                    nc.scalar.activation(XH[:, b * TOK:(b + 1) * TOK], PR[:, i, :], ACT.Copy).then_inc(s_xh, 1)
                act.wait_ge(s_gz, g + 1)
                nc.scalar.activation(GT[:, 1, :, :], GT[:, 0, :, :], ACT.Exp).then_inc(s_gez, 1)
                for k in range(4, E):
                    weight_hi(g * E + k)

            def gelus(b, first):
                for n in range(NCH):
                    slot = n % RING
                    done = b * NCH + n
                    act.wait_ge(s_pre, done + 1)
                    if not (first and n < RING):
                        act.wait_ge(s_used, done - RING + 1)
                    nc.scalar.activation(HF[:, slot, :], bank[slot][:], ACT.Gelu, bias=B1[:, n:n + 1])
                    nc.scalar.activation(HH[:, slot, :], bank[slot][:], ACT.Gelu,
                                         bias=B1[:, n:n + 1]).then_inc(s_gelu, 1)
                    if first and n == 24:
                        gates_store(NG - 1)

            gelus(0, True)
            with act.Fori(1, NB) as b:
                gelus(b, False)

        @block.tensor
        def _(pe):
            mm = nc.tensor.matmul
            pe.wait_ge(ld_mod, 32)
            pe.wait_ge(s_sil, 1)
            for k, col in ((0, 1), (1, 0)):
                last = mm(bank[0][:, k * NB:(k + 1) * NB], WMOD[:, col * P:(col + 1) * P], SIL[:, 3, :],
                          start=True, stop=True)
            last.then_inc(s_modp, 1)
            mm(bank[2][0:NB, :], SIL[:, 3, :], WMOD[:, 2 * P:6 * P], start=True, stop=True).then_inc(s_mod8p, 1)
            pe.wait_ge(s_const, 3)
            pe.wait_ge(s_bqv, 2)
            pe.wait_ge(ld_qv, 48)
            pe.wait_ge(s_modt, 1)

            def transposes(dst, src):
                for j in range(NJ):
                    last = nc.tensor.transpose(tok(dst, j), tok(src, j), IDENT[:])
                return last

            def gates_transpose(g):
                pe.wait_ge(s_w, g + 1)
                nc.tensor.transpose(gates_ps(g), GT[:, 3, :, :].rearrange("p a e -> p (a e)"), IDENT[:]).then_inc(s_wt, 1)

            for g in range(NG):
                for i in range(G):
                    n = g * G + i + 1
                    pe.wait_ge(s_xn1, n)
                    if i >= 2:
                        pe.wait_ge(s_h1, n - 2)
                    transposes(bank[i % 2], XN[:, i, :]).then_inc(s_xn1t, 1)
                if g == 0:
                    pe.wait_ge(s_mod8, 1)
                for i in range(G):
                    n = g * G + i + 1
                    pe.wait_ge(s_h1, n)
                    if i >= 2:
                        pe.wait_ge(s_qs, n - 2)
                        pe.wait_ge(s_vc, n - 2)
                    for k, done in ((0, s_q), (1, s_v)):
                        acc = bank[2 + 2 * k + i % 2]
                        mm(acc[:], ONESR[0:64, :], BQV[:, k:k + 1, :].to_broadcast([64, NJ, P]),
                           start=True, stop=False, skip_group_check=True)
                        for j in range(NJ):
                            last = mm(tok(acc, j), tok(HT[:, i, :], j), WQV[:, k, :], start=False,
                                      stop=(j == NJ - 1), skip_group_check=True)
                        last.then_inc(done, 1)
                if g > 0:
                    gates_transpose(g - 1)
                for i in range(G):
                    n = g * G + i + 1
                    pe.wait_ge(s_p, n)
                    if i >= 2:
                        pe.wait_ge(s_ptc, n - 2)
                    transposes(bank[2 + i % 2], PR[:, i, :]).then_inc(s_pt, 1)
                    pe.wait_ge(s_kx, n)
                    pe.wait_ge(s_vc, n)
                    if i >= 2:
                        pe.wait_ge(s_ct, n - 2)
                    ctx_ps = bank[i % 2]
                    for j in range(NJ):
                        mm(ctx_ps[:, 0:P], tok(V[:, i, :], j), tok(EX[:, i, :], j), start=(j == 0), stop=(j == NJ - 1))
                    for j in range(NJ):
                        last = mm(ctx_ps[:, P:P + 1], tok(EX[:, i, :], j), ONESR[:, 0:1].bitcast(F32), start=(j == 0),
                                  stop=(j == NJ - 1))
                    last.then_inc(s_ctx, 1)
                if g == 0:
                    pe.wait_ge(ld_small, 112)
                for i in range(G):
                    pe.wait_ge(s_ct, g * G + i + 1)
                    if i == 1:
                        pe.wait_ge(s_ptc, g * G + 3)
                    if i >= 2:
                        pe.wait_ge(s_ms, g * G + i - 1)
                    mm(bank[(6, 2)[i % 2]][:, 0:P], CTX[:, i, :], WO[:], start=True, stop=True).then_inc(s_m, 1)
                for i in range(G):
                    n = g * G + i + 1
                    pe.wait_ge(s_ms, n)
                    pe.wait_ge(s_ptc, n)
                    if i >= 2:
                        pe.wait_ge(s_x1, n - 2)
                    for j in range(NJ):
                        last = mm(tok(bank[4 + i % 2], j), tok(HT[:, i, :], j), MS[:, i, :], start=True, stop=True)
                    last.then_inc(s_att, 1)
                for i in range(G):
                    n = g * G + i + 1
                    pe.wait_ge(s_xn3, n)
                    if i >= 2:
                        pe.wait_ge(s_xf, n - 2)
                    transposes(bank[i % 2], XN[:, i, :]).then_inc(s_xn3t, 1)
                if g > 0:
                    pe.wait_ge(s_wtc, g)
                mm(logits_ps(g), ONESR[0:1, :].bitcast(F32), BG[:].unsqueeze(1).to_broadcast([1, G * NJ, E]), start=True,
                   stop=False, skip_group_check=True)
                for i in range(G):
                    pe.wait_ge(s_xf, g * G + i + 1)
                    for j in range(NJ):
                        a = i * NJ + j
                        last = mm(logits_ps(g)[:, a * E:(a + 1) * E], tok(PR[:, i, :], j), WG[:], start=False,
                                  stop=(a == G * NJ - 1), skip_group_check=True)
                last.then_inc(s_lg, 1)

            pe.wait_ge(s_xl, NB)

            def first_product(b, n, first):
                done = b * NCH + n
                e, c = n // CH, n % CH
                if first and c == 0:
                    pe.wait_ge(s_wl, 2 * (e + 1))
                if not (first and n < RING):
                    pe.wait_ge(s_gelu, done - RING + 1)
                w = slice(e * 1024 + c * P, e * 1024 + (c + 1) * P)
                xs = ds(b * TOK, TOK)
                mm(bank[n % RING][:], WH[:, w], XH[:, xs], start=True, stop=False)
                mm(bank[n % RING][:], WH[:, w], XL[:, xs], start=False, stop=False)
                mm(bank[n % RING][:], WL[:, w], XH[:, xs], start=False, stop=True).then_inc(s_pre, 1)

            def second_product(b, n, first):
                done = b * NCH + n
                e, c, slot = n // CH, n % CH, n % RING
                y = bank[4 + e % 2]
                if c == 0 and not (first and e < 2):
                    pe.wait_ge(s_yread, b * E + e - 1)
                w = slice(e * 1024 + 512 + c * P, e * 1024 + 512 + (c + 1) * P)
                pe.wait_ge(s_gelu, done + 1)
                mm(y[:], WH[:, w], HH[:, slot, :], start=(c == 0), stop=False)
                mm(y[:], WL[:, w], HH[:, slot, :], start=False, stop=False)
                pe.wait_ge(s_hl, done + 1)
                mm(y[:], WH[:, w], HL[:, slot, :], start=False, stop=(c == CH - 1)).then_inc(s_used, 1)

            def output_transposes(b):
                pe.wait_ge(s_yt, b + 1)
                transposes(bank[6], YT).then_inc(s_ytt, 1)

            def experts(b, first):
                for n in range(NCH):
                    first_product(b, n, first)
                    if n >= LAG:
                        second_product(b, n - LAG, first)
                    elif not first:
                        second_product(b - 1, n - LAG + NCH, False)
                    if n == 7 and not first:
                        output_transposes(b - 1)
                    if n == 23 and first:
                        gates_transpose(NG - 1)

            experts(0, True)
            with pe.Fori(1, NB) as b:
                experts(b, False)
            for n in range(NCH - LAG, NCH):
                second_product(NB - 1, n, False)
            output_transposes(NB - 1)

        @block.vector
        def _(dve):
            v = nc.vector
            v.memset(BRAW[:], 0.0).then_inc(s_zero, 1)
            for e in range(E):
                last = v.memset(RANK[:, e:e + 1], float(E - e))
            last.then_inc(s_dset, 1)
            dve.wait_ge(s_es, 1)
            dve.wait_ge(ld_mod, 32)
            v.tensor_scalar(SIL[:, 1, :], SIL[:, 0, :], 1.0, None, ALU.add).then_inc(s_dset, 1)
            dve.wait_ge(s_dset, 2)
            v.reciprocal(SIL[:, 2, :], SIL[:, 1, :]).then_inc(s_dset, 1)
            dve.wait_ge(s_dset, 3)
            v.tensor_tensor(SIL[:, 3, :], CT[:], SIL[:, 2, :], ALU.mult).then_inc(s_sil, 1)

            def stats(k, b, src):
                for j in range(NJ):
                    last = v.bn_stats(ST[:, k, b * NJ + j, :], tok(src, j))
                last.then_inc(s_st[k], 1)
                dve.wait_ge(s_st[k], b + 1)
                for j in range(NJ):
                    last = v.bn_aggr(MV[:, k, b * NJ + j, :], ST[:, k, b * NJ + j, :])
                last.then_inc(s_mv[k], 1)

            def shift(k, b):
                at = slice(b * NJ, (b + 1) * NJ)
                dve.wait_ge(s_rstd[k], b + 1)
                v.scalar_tensor_tensor(out=NMR[:, k, at], in0=MV[:, k, at, 0], scalar=-1.0, in1=RSTD[:, k, at],
                                       op0=ALU.mult, op1=ALU.mult).then_inc(s_nmr[k], 1)

            def modulation_columns():
                dve.wait_ge(s_modp, 1)
                v.tensor_scalar(MODT[:, 0, :], bank[0][:, 0:NB], 1.0, None, ALU.add)
                v.tensor_copy(MODT[:, 1, :], bank[0][:, NB:2 * NB]).then_inc(s_modt, 1)

            def bias_split():
                dve.wait_ge(ld_qv, 48)
                dve.wait_ge(s_const, 1)
                v.tensor_copy(ONESR[:], ONES[:]).then_inc(s_bqv, 1)
                v.tensor_copy(BQV[:], BRAW[:]).then_inc(s_dset, 1)
                dve.wait_ge(s_dset, 4)
                v.tensor_tensor(BQV[32:64, :, :], BRAW[32:64, :, :], BQV[32:64, :, :].bitcast(F32),
                                ALU.subtract).then_inc(s_bqv, 1)

            def modulation_rows():
                dve.wait_ge(s_mod8p, 1)
                v.tensor_copy(MOD8[:, 0:4, :], bank[2][0:NB, :].rearrange("p (r n) -> p r n", r=4)).then_inc(s_dset, 1)
                dve.wait_ge(s_dset, 5)
                g8 = MOD8[:, 0:4:3, :]
                v.scalar_tensor_tensor(out=MAG8[:, 0, :, :], in0=g8, scalar=-1.0, in1=g8, op0=ALU.mult,
                                       op1=ALU.max).then_inc(s_dset, 1)
                v.tensor_scalar(MAG8[:, 1, :, :], g8, 0.0, 2.0, ALU.is_ge, ALU.mult).then_inc(s_dset, 1)
                v.tensor_scalar(MOD8[:, 2, :], MOD8[:, 2, :], 1.0, None, ALU.add).then_inc(s_dset, 1)
                dve.wait_ge(s_dset, 8)
                v.tensor_scalar(MAG8[:, 2, :, :], MAG8[:, 0, :, :], 0.25, None, ALU.max).then_inc(s_dset, 1)
                dve.wait_ge(s_dset, 9)
                v.scalar_tensor_tensor(out=g8, in0=MAG8[:, 1, :, :], scalar=1.0, in1=MAG8[:, 2, :, :],
                                       op0=ALU.subtract, op1=ALU.mult).then_inc(s_dset, 1)
                dve.wait_ge(s_dset, 10)
                dve.wait_ge(ld_small, 112)
                v.tensor_tensor(MOD8[:, 4, :], MOD8[:, 0, :], BO[:], ALU.mult).then_inc(s_mod8, 1)

            for b in range(NB):
                dve.wait_ge(ld_x[b], 16)
                stats(0, b, X[:, b * TOK:(b + 1) * TOK])
                if b == 1:
                    modulation_columns()
                if b >= 2:
                    shift(0, b - 2)
                if b == 3:
                    bias_split()
                if b == 5:
                    modulation_rows()
            shift(0, NB - 2)
            shift(0, NB - 1)

            z, ez, first_hot, rest, second_hot = (GT[:, k, :, :] for k in range(5))
            pr, eq, w = z, ez, rest
            top, total, inv, best, rank1, second, rank2, scale = (GS[:, k, :] for k in range(8))
            linked = [0]

            def wide(t):
                return t.unsqueeze(2).to_broadcast([P, G * NJ, E])

            def link(ins):
                linked[0] += 1
                ins.then_inc(s_gate, 1)
                dve.wait_ge(s_gate, linked[0])

            def gates_shift(g):
                dve.wait_ge(s_lg, g + 1)
                logits = logits_ps(g).rearrange("p (a e) -> p a e", e=E)
                link(v.tensor_reduce(top, logits, AX.X, ALU.max))
                v.tensor_tensor(z, logits, wide(top), ALU.subtract).then_inc(s_gz, 1)

            def gates_softmax(g):
                dve.wait_ge(s_gez, g + 1)
                link(v.tensor_reduce(total, ez, AX.X, ALU.add))
                link(v.reciprocal(inv, total))
                link(v.tensor_tensor(pr, ez, wide(inv), ALU.mult))

            def gates_first(g):
                link(v.tensor_reduce(best, pr, AX.X, ALU.max))
                link(v.tensor_tensor(eq, pr, wide(best), ALU.is_equal))
                link(v.tensor_tensor(eq, eq, RANK[:].unsqueeze(1).to_broadcast([P, G * NJ, E]), ALU.mult))
                link(v.tensor_reduce(rank1, eq, AX.X, ALU.max))
                link(v.tensor_tensor(first_hot, eq, wide(rank1), ALU.is_equal))

            def gates_second(g):
                if g > 0:
                    dve.wait_ge(s_wt, g)
                link(v.scalar_tensor_tensor(out=rest, in0=first_hot, scalar=-2.0, in1=pr, op0=ALU.mult, op1=ALU.add))
                link(v.tensor_reduce(second, rest, AX.X, ALU.max))
                link(v.tensor_tensor(eq, rest, wide(second), ALU.is_equal))
                link(v.tensor_tensor(eq, eq, RANK[:].unsqueeze(1).to_broadcast([P, G * NJ, E]), ALU.mult))
                link(v.tensor_reduce(rank2, eq, AX.X, ALU.max))
                link(v.tensor_tensor(second_hot, eq, wide(rank2), ALU.is_equal))

            def gates_scale(g):
                link(v.tensor_tensor(first_hot, first_hot, second_hot, ALU.add))
                link(v.tensor_tensor(scale, best, second, ALU.add))
                link(v.tensor_scalar(scale, scale, EPS_TOPK, None, ALU.add))
                link(v.reciprocal(scale, scale))
                link(v.tensor_tensor(w, pr, first_hot, ALU.mult))
                v.tensor_tensor(w, w, wide(scale), ALU.mult).then_inc(s_w, 1)

            for g in range(NG):
                def xb(i):
                    return X[:, ds((g * G + i) * TOK, TOK)]

                if g > 0:
                    gates_softmax(g - 1)
                    gates_first(g - 1)
                    gates_second(g - 1)
                    gates_scale(g - 1)
                for i in range(G):
                    n = g * G + i + 1
                    q = bank[2 + i % 2][:].rearrange(heads, k=DH)
                    dve.wait_ge(s_q, n)
                    v.tensor_reduce(SM[:, i % 2, 0, :], q, AX.X, ALU.max).then_inc(s_mx, 1)
                    dve.wait_ge(s_mx, n)
                    v.tensor_tensor(EX[:, i, :].rearrange(heads, k=DH), q,
                                    SM[:, i % 2, 0, :].unsqueeze(2).to_broadcast([P, HEADS * NJ, DH]),
                                    ALU.subtract).then_inc(s_qs, 1)
                for i in range(G):
                    n = g * G + i + 1
                    ex = EX[:, i, :].rearrange(heads, k=DH)
                    dve.wait_ge(s_e, n)
                    v.tensor_reduce(SM[:, i % 2, 1, :], ex, AX.X, ALU.add).then_inc(s_sm, 1)
                    dve.wait_ge(s_sm, n)
                    if n > 2:
                        dve.wait_ge(s_p, n - 2)
                    v.reciprocal(SM[:, i % 2, 2, :], SM[:, i % 2, 1, :]).then_inc(s_rc, 1)
                    dve.wait_ge(s_rc, n)
                    if g == 0 and i == 0:
                        dve.wait_ge(s_mod8p, 1)
                        dve.wait_ge(st_mod, 16)
                    v.tensor_tensor(PR[:, i, :].rearrange(heads, k=DH), ex,
                                    SM[:, i % 2, 2, :].unsqueeze(2).to_broadcast([P, HEADS * NJ, DH]),
                                    ALU.mult).then_inc(s_p, 1)
                for i in range(G):
                    dve.wait_ge(s_ctx, g * G + i + 1)
                    v.tensor_tensor(CTX[:, i, :], bank[i % 2][:, 0:P], HMASK[:].rearrange("p m k -> p (m k)"),
                                    ALU.mult)
                    v.reciprocal(RDEN[:, i, :], bank[i % 2][:, P:P + 1]).then_inc(s_ct, 1)
                if g == 0:
                    dve.wait_ge(ld_rows, 16)
                for i in range(G):
                    dve.wait_ge(s_m, g * G + i + 1)
                    v.scalar_tensor_tensor(out=MS[:, i, :], in0=bank[(6, 2)[i % 2]][:, 0:P], scalar=RDEN[:, i, 0:1],
                                           in1=ROWS[:, ds(g * G + i, 1), 0, :].rearrange("p b n -> p (b n)"),
                                           op0=ALU.mult, op1=ALU.mult).then_inc(s_ms, 1)
                for i in range(G):
                    n = g * G + i + 1
                    dve.wait_ge(s_att, n)
                    dve.wait_ge(s_xg, n)
                    v.tensor_tensor(xb(i), bank[4 + i % 2][:], xb(i), ALU.add).then_inc(s_x1, 1)
                    dve.wait_ge(s_x1, n)
                    stats(1, g * G + i, xb(i))
                for i in range(G):
                    b = g * G + i
                    dve.wait_ge(s_rstd[1], b + 1)
                    for j in range(NJ):
                        a = b * NJ + j
                        last = v.tensor_scalar(tok(XN[:, i, :], j), tok(xb(i), j), MV[:, 1, a, 0:1],
                                               RSTD[:, 1, a:a + 1], ALU.subtract, ALU.mult)
                    last.then_inc(s_xn2, 1)
                for i in range(G):
                    n = g * G + i + 1
                    h2 = V[:, i, :].rearrange("p (j d) -> p j d", j=NJ)
                    dve.wait_ge(s_t2, n)
                    v.tensor_tensor(h2, h2, ROWS[:, ds(g * G + i, 1), 1, :].to_broadcast([P, NJ, P]),
                                    ALU.add).then_inc(s_h2, 1)
                    dve.wait_ge(s_h2, n)
                    stats(2, g * G + i, V[:, i, :])
                for i in range(G):
                    shift(2, g * G + i)
                for i in range(G):
                    n = g * G + i + 1
                    at = ds((g * G + i) * TOK, TOK)
                    dve.wait_ge(s_xh, n)
                    v.tensor_tensor(XL[:, at], PR[:, i, :], XH[:, at].bitcast(F32), ALU.subtract).then_inc(s_xl, 1)
                gates_shift(g)

            def lo(b, n, first):
                slot = n % RING
                done = b * NCH + n
                dve.wait_ge(s_gelu, done + 1)
                if not (first and n < RING):
                    dve.wait_ge(s_used, done - RING + 1)
                v.tensor_tensor(HL[:, slot, :], HF[:, slot, :], HH[:, slot, :].bitcast(F32),
                                ALU.subtract).then_inc(s_hl, 1)

            def gated(b, e):
                done = b * E + e
                dve.wait_ge(s_used, done * CH + CH)
                dve.wait_ge(ld_wb[e], (b + 1) * 16)
                y = bank[4 + e % 2][:]
                v.scalar_tensor_tensor(out=ACC if e == 0 else YW, in0=y, scalar=B2[:, e:e + 1], in1=WB[:, e, :],
                                       op0=ALU.add, op1=ALU.mult).then_inc(s_yread, 1)
                if e == 0:
                    return
                dve.wait_ge(s_yread, done + 1)
                if e > 1:
                    dve.wait_ge(s_acc, b * (E - 2) + e - 1)
                if e < E - 1:
                    v.tensor_tensor(ACC, ACC, YW, ALU.add).then_inc(s_acc, 1)
                else:
                    v.tensor_tensor(YT, ACC, YW, ALU.add).then_inc(s_yt, 1)

            def result(b):
                dve.wait_ge(s_ytt, b + 1)
                v.tensor_tensor(OT.rearrange("p (j d) -> p j d", j=NJ), bank[6][:].rearrange("p (j d) -> p j d", j=NJ),
                                ROWS[:, ds(b, 1), 3, :].to_broadcast([P, NJ, P]), ALU.mult).then_inc(s_o1, 1)
                dve.wait_ge(s_o1, b + 1)
                xr = X[:, ds(b * TOK, TOK)]
                v.tensor_tensor(xr, xr, OT, ALU.add).then_inc(s_res2, 1)

            def experts(b, first):
                for n in range(NCH):
                    lo(b, n, first)
                    if n % CH == 1 and n > CH:
                        gated(b, n // CH - 1)
                    if n == 1 and not first:
                        gated(b - 1, E - 1)
                    if n == 11 and not first:
                        result(b - 1)
                    if first and n == 10:
                        gates_softmax(NG - 1)
                    if first and n == 13:
                        gates_first(NG - 1)
                    if first and n == 16:
                        gates_second(NG - 1)
                    if first and n == 19:
                        gates_scale(NG - 1)

            experts(0, True)
            dve.wait_ge(s_res, NB)
            with dve.Fori(1, NB) as b:
                experts(b, False)
            gated(NB - 1, E - 1)
            result(NB - 1)


def kernel(**inputs):
    import numpy as _np
    import concourse.bacc as _bacc
    from concourse.bass_utils import run_bass_kernel_spmd as _run

    a = {k: _np.asarray(v) for k, v in inputs.items()}
    d, e, f = P, E, CH * P
    w1 = a["L0_ffn_W1"].transpose(2, 0, 1)
    w2 = a["L0_ffn_W2"].transpose(0, 2, 1).reshape(e, CH, P, d).transpose(2, 0, 1, 3).reshape(P, e, CH * d)
    arrays = {
        "x": a["L0_attn_x"],
        "wqv": _np.stack([a["L0_attn_Wq"], a["L0_attn_Wv"]], axis=1), "wo": a["L0_attn_Wo"],
        "bqv": _np.stack([a["L0_attn_bq"], a["L0_attn_bv"]])[None], "bo": a["L0_attn_bo"].reshape(1, d),
        "gb": _np.stack([a["L0_ffn_gamma"], a["L0_ffn_beta"]], axis=1),
        "wg": a["L0_ffn_Wg"].T, "bg": a["L0_ffn_bg"].reshape(1, e),
        "w12": _np.stack([w1, w2], axis=2).reshape(P, 2 * e * f),
        "b1": a["L0_ffn_b1"].reshape(e * CH, P).T, "b2": a["L0_ffn_b2"].T,
        "c_t": a["L0_c"].T, "wmod": a["L0_wmod"],
    }
    arrays = {k: _np.ascontiguousarray(v) for k, v in arrays.items()}
    nc = _bacc.Bacc("TRN2", target_bir_lowering=False, num_devices=1)
    args = {k: nc.dram_tensor(k, v.shape, F32, kind="ExternalInput").ap() for k, v in arrays.items()}
    mod_dram = nc.dram_tensor("mod_dram", (NB, 5, P), F32).ap()
    w_dram = nc.dram_tensor("w_dram", (NB, NJ, E, P), F32).ap()
    out = nc.dram_tensor("out", (NB, TOK, P), F32, kind="ExternalOutput").ap()
    adaln_block(nc, mod_dram=mod_dram, w_dram=w_dram, out=out, **args)
    r = _run(nc, [arrays], core_ids=[0])
    return r.results[0]["out"]
```

```python
from contextlib import ExitStack

import concourse.bass as bass
from concourse import mybir

F32 = mybir.dt.float32
F32R = mybir.dt.float32r
ACT = mybir.ActivationFunctionType
ALU = mybir.AluOpType
AX = mybir.AxisListType

P = 128
NB = 8
NJ = 4
TOK = P * NJ
G = 4
NG = NB // G
HEADS, DH = 16, 8
E = 8
CH = 4
NCH = E * CH
LAG = 3
RING = 4
LEAD = 6
STAGES = 31
STEPS = (NB - 1) * LEAD + STAGES
B_STEP = (NB - 1) * LEAD + 18
EARLY = 1
GATES_STEP = (G - 1) * LEAD + 28
SPLIT_EARLY = 8
GATES_CHAIN = 20
GATES_PER_STEP = 4
GATES_CHUNK = 13
EPS_LN = 1e-5
EPS_TOPK = 1e-8
S_QK = (DH ** 0.5) ** (-0.25)
ds = bass.ds


def adaln_block(nc, x, wqv, wo, bqv, bo, gb, wg, bg, w12, b1, b2, c_t, wmod, mod_dram, w_dram, out):
    with ExitStack() as ctx:
        def sb(name, shape, dt=F32):
            return ctx.enter_context(nc.sbuf_tensor(name, shape, dt))

        names = {}

        def sem(name):
            names[name] = ctx.enter_context(nc.semaphore(name))
            return names[name]

        X = sb("X", [P, NB * TOK])
        WH = sb("WH", [P, 2 * E * 512], F32R)
        WL = sb("WL", [P, 2 * E * 512], F32R)
        XH = sb("XH", [P, NB * TOK], F32R)
        XL = sb("XL", [P, NB * TOK], F32R)
        ROWS = sb("ROWS", [P, NB, 5, P])
        HH = sb("HH", [P, RING, TOK], F32R)
        HL = sb("HL", [P, RING, TOK], F32R)
        STAGE = sb("STAGE", [P, 2, 512])
        WQV = sb("WQV", [P, 2, P])
        WO = sb("WO", [P, P])
        WG = sb("WG", [P, E])
        B1 = sb("B1", [P, NCH])
        B2 = sb("B2", [P, E])
        GB = sb("GB", [P, 2])
        BQV = sb("BQV", [64, 2, P], F32R)
        ONESR = sb("ONESR", [P, P], F32R)
        BG = sb("BG", [1, E])
        CT = sb("CT", [P, NB])
        SIL = sb("SIL", [P, 4, NB])
        MODT = sb("MODT", [P, 2, NB])
        IDENT = sb("IDENT", [P, P])
        HMASK = sb("HMASK", [P, HEADS, DH])
        NHALF = sb("NHALF", [P, NJ])
        RANK = sb("RANK", [P, E])
        ST = sb("ST", [P, 3, NB * NJ, 6])
        MV = sb("MV", [P, 3, NB * NJ, 2])
        VE = sb("VE", [P, 3, NB * NJ])
        RSTD = sb("RSTD", [P, 3, NB * NJ])
        NMR = sb("NMR", [P, 3, NB * NJ])
        SM = sb("SM", [P, 2, 3, HEADS * NJ])
        CTX = sb("CTX", [P, G, P])
        RDEN = sb("RDEN", [P, 2, G])
        MS = CTX
        GT = sb("GT", [P, 5, G * NJ, E])
        GS = sb("GS", [P, 8, G * NJ])
        WT = sb("WT", [P, P])
        ARENA = sb("ARENA", [P, 5 * G * TOK])

        def area(k):
            return ARENA[:, k * G * TOK:(k + 1) * G * TOK].rearrange("p (i n) -> p i n", i=G)

        XN, HT, V, EX, PR = (area(k) for k in range(5))
        WMOD = ARENA[:, 4 * G * TOK:4 * G * TOK + 6 * P]
        MOD8 = ARENA[0:NB, 4 * G * TOK + 6 * P:4 * G * TOK + 11 * P].rearrange("p (r n) -> p r n", r=5)
        MAG8 = ARENA[0:NB, 3 * G * TOK:3 * G * TOK + 6 * P].rearrange("p (k r n) -> p k r n", k=3, r=2)
        BRAW = ARENA[0:64, 3 * G * TOK + 6 * P:3 * G * TOK + 8 * P].rearrange("p (k n) -> p k n", k=2)
        BO = ARENA[0:NB, 3 * G * TOK + 8 * P:3 * G * TOK + 9 * P]
        ONES = ARENA[:, 3 * G * TOK + 9 * P:3 * G * TOK + 10 * P]
        HF = HT
        ACC, YW, YT, OT = (XN[:, k, :] for k in range(4))
        WB = ARENA[:, 3 * G * TOK:3 * G * TOK + E * TOK].rearrange("p (e n) -> p e n", e=E)

        bank = [ctx.enter_context(nc.psum_tensor(f"bank{k}", [P, 512], F32)) for k in range(8)]

        ld_x = [sem(f"ld_x{b}") for b in range(NB)]
        ld_mod, ld_qv, ld_small, ld_rows = sem("ld_mod"), sem("ld_qv"), sem("ld_small"), sem("ld_rows")
        ld_w = [sem("ld_w0"), sem("ld_w1")]
        s_const, s_pc, s_zero, s_es, s_sil, s_bqv, s_modp, s_modt, s_mod8p, s_mod8, s_dset, st_mod = (
            sem(n) for n in ("s_const", "s_pc", "s_zero", "s_es", "s_sil", "s_bqv", "s_modp", "s_modt", "s_mod8p",
                             "s_mod8", "s_dset", "st_mod"))
        (s_st, s_mv, s_ve, s_rstd) = ([sem(f"{n}{k}") for k in range(3)] for n in ("s_st", "s_mv", "s_ve", "s_rstd"))
        s_nmr = {k: sem(f"s_nmr{k}") for k in (0, 2)}
        (s_xn1, s_msa, s_xn1t, s_h1, s_q, s_v, s_mx, s_qs, s_vc, s_e, s_sm, s_rc, s_p, s_kx, s_pt, s_ptc, s_ctx, s_ct,
         s_m, s_ms, s_att, s_x1, s_cen, s_h2, s_xn3, s_xn3t, s_xf, s_xh, s_xl, s_lg, s_wt, s_wtc,
         s_r1, s_res) = (sem(n) for n in (
             "s_xn1", "s_msa", "s_xn1t", "s_h1", "s_q", "s_v", "s_mx", "s_qs", "s_vc", "s_e", "s_sm", "s_rc", "s_p",
             "s_kx", "s_pt", "s_ptc", "s_ctx", "s_ct", "s_m", "s_ms", "s_att", "s_x1", "s_cen", "s_h2",
             "s_xn3", "s_xn3t", "s_xf", "s_xh", "s_xl", "s_lg", "s_wt", "s_wtc", "s_r1", "s_res"))
        s_qc, s_top, s_gz, s_gez, s_gate, s_w = (
            sem(n) for n in ("s_qc", "s_top", "s_gz", "s_gez", "s_gate", "s_w"))
        s_wh, s_wl = sem("s_wh"), sem("s_wl")
        st_w = [sem("st_w0"), sem("st_w1")]
        s_pre, s_gelu, s_hl, s_used, s_yread, s_acc, s_yt, s_ytt, s_o1, s_res2, st_out = (
            sem(n) for n in ("s_pre", "s_gelu", "s_hl", "s_used", "s_yread", "s_acc", "s_yt", "s_ytt", "s_o1",
                             "s_res2", "st_out"))
        ld_wb = [sem(f"ld_wb{e}") for e in range(E)]

        block = ctx.enter_context(nc.Block())

        x_p = x.rearrange("b (p j) d -> p b (j d)", j=NJ)
        out_p = out.rearrange("b (p j) d -> p b (j d)", j=NJ)
        heads = "p (m k) -> p m k"

        def tok(t, j):
            return t[:, j * P:(j + 1) * P]

        def per_token(t):
            return t.rearrange("p (j d) -> p j d", j=NJ)

        def at_step(t, engine_stages):
            for b in range(NB):
                stage = engine_stages.get(t - b * LEAD)
                if stage is not None:
                    stage(b)

        def first_statistics(t):
            return [t + 1] if t < NB - 1 else []

        def early_chunks(t):
            return range(EARLY * (t - B_STEP), EARLY * (t - B_STEP + 1)) if t >= B_STEP else range(0)

        LATE = EARLY * (STEPS - B_STEP)

        def weights_of_step(t):
            k = (t - 12) // 6
            return [k] if (t - 12) % 6 == 0 and 0 <= k < SPLIT_EARLY else []

        def xs(b):
            return slice(b * TOK, (b + 1) * TOK)

        @block.sync
        def _(sp):
            sp.dma_start(CT[:], c_t).then_inc(ld_mod, 16)
            sp.dma_start(WMOD, wmod).then_inc(ld_mod, 16)
            for b in range(NB):
                if b == 2:
                    sp.dma_start(WQV[:], wqv).then_inc(ld_qv, 16)
                sp.dma_start(X[:, b * TOK:(b + 1) * TOK], x_p[:, b, :]).then_inc(ld_x[b], 16)

            def weight_load(k):
                if k >= 2:
                    sp.wait_ge(s_wl, k - 1)
                sp.dma_start(STAGE[:, k % 2, :], w12[:, k * 512:(k + 1) * 512]).then_inc(ld_w[k % 2], 16)

            def gates_load(e):
                sp.dma_start(per_token(WB[:, e, :]),
                             w_dram[0:1, :, e, :].to_broadcast([P, NJ, P])).then_inc(ld_wb[e], 16)

            weight_load(0)
            weight_load(1)
            sp.wait_ge(s_mod8, 1)
            sp.dma_start(mod_dram, MOD8[:]).then_inc(st_mod, 16)
            sp.wait_ge(st_mod, 16)
            sp.dma_start(ROWS[:], mod_dram.unsqueeze(0).to_broadcast([P, NB, 5, P])).then_inc(ld_rows, 16)
            for k in range(2, SPLIT_EARLY + 1):
                weight_load(k)
            sp.wait_ge(st_w[0], 16)
            sp.wait_ge(s_ct, NB)
            for e in range(E // 2):
                gates_load(e)
            weight_load(SPLIT_EARLY + 1)
            sp.wait_ge(s_lg, NB)
            sp.wait_ge(s_xl, NB)
            for e in range(E // 2, E):
                gates_load(e)
                weight_load(SPLIT_EARLY + 2 + e - E // 2)
            for k in range(SPLIT_EARLY + 2 + E // 2, 2 * E):
                weight_load(k)
            sp.wait_ge(st_w[1], 16)
            with sp.Fori(1, NB) as b:
                for e in range(E):
                    sp.wait_ge(s_yread, (b - 1) * E + e + 1)
                    sp.dma_start(per_token(WB[:, e, :]),
                                 w_dram[ds(b, 1), :, e, :].to_broadcast([P, NJ, P])).then_inc(ld_wb[e], 16)
                    if e == 3:
                        sp.wait_ge(s_res2, b)
                        sp.dma_start(out_p[:, ds(b - 1, 1), :], X[:, ds((b - 1) * TOK, TOK)]).then_inc(st_out, 16)
            sp.wait_ge(s_res2, NB)
            sp.dma_start(out_p[:, NB - 1, :], X[:, (NB - 1) * TOK:NB * TOK]).then_inc(st_out, 16)
            sp.wait_ge(st_out, 16 * NB)

        @block.gpsimd
        def _(pool):
            pl = nc.gpsimd
            pl.memset(IDENT[:], 0.0).then_inc(s_pc, 1)
            pl.memset(HMASK[:], S_QK * S_QK).then_inc(s_pc, 1)
            pl.memset(NHALF[:], -0.5).then_inc(s_pc, 1)
            pl.memset(ONES[:], 1.0).then_inc(s_const, 1)
            pool.wait_ge(s_pc, 3)
            pl.affine_select(out=IDENT[:], in_=IDENT[:], compare_op=ALU.not_equal, fill=1.0, base=0,
                             pattern=[[-1, P]], channel_multiplier=1).then_inc(s_const, 1)
            pl.affine_select(out=HMASK[:], in_=HMASK[:], compare_op=ALU.is_ge, fill=0.0, base=0,
                             pattern=[[-DH, HEADS], [0, DH]], channel_multiplier=1).then_inc(s_pc, 1)
            pool.wait_ge(s_pc, 4)
            pl.affine_select(out=HMASK[:], in_=HMASK[:], compare_op=ALU.is_ge, fill=0.0, base=DH - 1,
                             pattern=[[DH, HEADS], [0, DH]], channel_multiplier=-1).then_inc(s_const, 1)

            def rstd(k, b):
                at = slice(b * NJ, (b + 1) * NJ)
                pool.wait_ge(s_mv[k], b + 1)
                pl.tensor_scalar(VE[:, k, at], MV[:, k, at, 1], EPS_LN, None, ALU.add).then_inc(s_ve[k], 1)
                pool.wait_ge(s_ve[k], b + 1)
                pl.tensor_tensor(RSTD[:, k, at], VE[:, k, at], NHALF[:], ALU.pow).then_inc(s_rstd[k], 1)

            def weight_lo(k):
                pool.wait_ge(s_wh, k + 1)
                at = slice(k * 512, (k + 1) * 512)
                pl.tensor_tensor(WL[:, at], STAGE[:, k % 2, :], WH[:, at].bitcast(F32), ALU.subtract).then_inc(s_wl, 1)

            def first_norm(b):
                rstd(0, b)

            def normalise_heads(b):
                pool.wait_ge(s_rc, b + 1)
                if b == 0:
                    pool.wait_ge(s_mod8p, 1)
                    pool.wait_ge(st_mod, 16)
                if b >= G:
                    pool.wait_ge(s_lg, b - G + 1)
                    pool.wait_ge(s_xl, b - G + 1)
                pl.tensor_tensor(PR[:, b % G, :].rearrange(heads, k=DH), EX[:, b % G, :].rearrange(heads, k=DH),
                                 SM[:, b % 2, 2, :].unsqueeze(2).to_broadcast([P, HEADS * NJ, DH]),
                                 ALU.mult).then_inc(s_p, 1)

            def second_norm(b):
                rstd(1, b)

            def third_norm(b):
                rstd(2, b)

            def residual(b):
                h2 = per_token(V[:, b % G, :])
                pool.wait_ge(s_xn3, b + 1)
                pl.tensor_tensor(h2, h2, ROWS[:, b:b + 1, 3, :].to_broadcast([P, NJ, P]), ALU.mult).then_inc(s_r1, 1)
                pool.wait_ge(s_r1, b + 1)
                pl.tensor_tensor(X[:, xs(b)], X[:, xs(b)], V[:, b % G, :], ALU.add).then_inc(s_res, 1)

            def input_lo(b):
                pool.wait_ge(s_xh, b + 1)
                pl.tensor_tensor(XL[:, xs(b)], PR[:, b % G, :], XH[:, xs(b)].bitcast(F32),
                                 ALU.subtract).then_inc(s_xl, 1)

            stages = {10: normalise_heads, 17: second_norm, 20: third_norm, 27: residual, 30: input_lo}
            first_norm(0)
            for t in range(STEPS):
                at_step(t, stages)
                for b in first_statistics(t):
                    first_norm(b)
                for k in weights_of_step(t):
                    weight_lo(k)
            for k in range(SPLIT_EARLY, 2 * E):
                at = slice(k * 512, (k + 1) * 512)
                pool.wait_ge(ld_w[k % 2], (k // 2 + 1) * 16)
                pl.tensor_copy(WH[:, at], STAGE[:, k % 2, :]).then_inc(s_wh, 1)
                weight_lo(k)

        @block.scalar
        def _(act):
            act.wait_ge(s_zero, 1)
            for part in (0, 32):
                act.dma_start(BRAW[part:part + 1, :, :], bqv).then_inc(ld_qv, 16)
            act.wait_ge(ld_mod, 32)
            nc.scalar.activation(SIL[:, 0, :], CT[:], ACT.Exp, scale=-1.0).then_inc(s_es, 1)
            for dst, src in ((WO[:], wo), (WG[:], wg), (B1[:], b1), (B2[:], b2), (GB[:], gb),
                             (BO[:], bo.to_broadcast([NB, P])), (BG[:], bg)):
                act.dma_start(dst, src).then_inc(ld_small, 16)

            def norm(k, b, src, done):
                act.wait_ge(s_nmr[k], b + 1)
                for j in range(NJ):
                    a = b * NJ + j
                    last = nc.scalar.activation(tok(XN[:, b % G, :], j), tok(src, j), ACT.Identity,
                                                bias=NMR[:, k, a:a + 1], scale=RSTD[:, k, a:a + 1])
                last.then_inc(done, 1)

            def weight_hi(k):
                act.wait_ge(ld_w[k % 2], (k // 2 + 1) * 16)
                nc.scalar.activation(WH[:, k * 512:(k + 1) * 512], STAGE[:, k % 2, :], ACT.Copy).then_inc(s_wh, 1)

            def gates_store(g):
                act.wait_ge(s_wt, g + 1)
                if g > 0:
                    act.wait_ge(st_w[g - 1], 16)
                nc.scalar.activation(WT[:], bank[7][:, 0:P], ACT.Copy).then_inc(s_wtc, 1)
                act.wait_ge(s_wtc, g + 1)
                act.dma_start(w_dram[g * G:(g + 1) * G].rearrange("b j e p -> (b j e) p"), WT[:]).then_inc(st_w[g], 16)

            def first_norm(b):
                if b >= G:
                    act.wait_ge(s_xn3t, b - G + 1)
                norm(0, b, X[:, xs(b)], s_xn1)

            def modulate(b):
                if b == 0:
                    act.wait_ge(s_modt, 1)
                act.wait_ge(s_xn1t, b + 1)
                nc.scalar.activation(HT[:, b % G, :], bank[0][:], ACT.Identity, bias=MODT[:, 1, b:b + 1],
                                     scale=MODT[:, 0, b:b + 1]).then_inc(s_h1, 1)

            def exponentials(b):
                act.wait_ge(s_v, b + 1)
                if b >= G:
                    act.wait_ge(s_res, b - G + 1)
                nc.scalar.activation(V[:, b % G, :], bank[4][:], ACT.Copy).then_inc(s_vc, 1)
                act.wait_ge(s_qs, b + 1)
                nc.scalar.activation(EX[:, b % G, :], EX[:, b % G, :], ACT.Exp).then_inc(s_e, 1)

            def keys(b):
                act.wait_ge(s_p, b + 1)
                nc.scalar.activation(EX[:, b % G, :], PR[:, b % G, :], ACT.Exp, scale=S_QK).then_inc(s_kx, 1)

            def queries(b):
                act.wait_ge(s_pt, b + 1)
                nc.scalar.activation(HT[:, b % G, :], bank[3][:], ACT.Copy).then_inc(s_qc, 1)
                act.wait_ge(s_qc, b + 1)
                nc.scalar.activation(bank[3][:], bank[3][:], ACT.Exp, scale=S_QK,
                                     accum_out=RDEN[:, 0, b % G:b % G + 1]).then_inc(s_ptc, 1)

            def third_norm(b):
                norm(2, b, V[:, b % G, :], s_xn3)

            def experts_input(b):
                if b == 0:
                    act.wait_ge(ld_small, 112)
                act.wait_ge(s_xn3t, b + 1)
                nc.scalar.activation(PR[:, b % G, :], bank[7][:], ACT.Identity,
                                     bias=GB[:, 1:2], scale=GB[:, 0:1]).then_inc(s_xf, 1)
                act.wait_ge(s_xf, b + 1)
                nc.scalar.activation(XH[:, xs(b)], PR[:, b % G, :], ACT.Copy).then_inc(s_xh, 1)

            def gates_exp(g):
                act.wait_ge(s_gz, (g + 1) * G)
                nc.scalar.activation(GT[:, 1, :, :], GT[:, 0, :, :], ACT.Exp).then_inc(s_gez, 1)

            def gelus(b, chunks, first):
                for n in chunks:
                    slot = n % RING
                    done = b * NCH + n
                    act.wait_ge(s_pre, done + 1)
                    if not (first and n < RING):
                        act.wait_ge(s_used, done - RING + 1)
                    if first and n == 0:
                        act.wait_ge(s_att, NB)
                    nc.scalar.activation(HF[:, slot, :], bank[slot][:], ACT.Gelu, bias=B1[:, n:n + 1])
                    nc.scalar.activation(HH[:, slot, :], bank[slot][:], ACT.Gelu,
                                         bias=B1[:, n:n + 1]).then_inc(s_gelu, 1)
                    if first and n == LATE + 1:
                        gates_exp(NG - 1)
                    if first and n == LATE + 17:
                        gates_store(NG - 1)

            stages = {4: first_norm, 6: modulate, 8: exponentials, 11: keys, 12: queries, 23: third_norm,
                      25: experts_input}
            for t in range(STEPS):
                at_step(t, stages)
                if t == GATES_STEP:
                    gates_exp(0)
                if t == GATES_STEP + 7:
                    gates_store(0)
                for k in weights_of_step(t):
                    weight_hi(k)
                gelus(0, early_chunks(t), True)
            gelus(0, range(LATE, NCH), True)
            with act.Fori(1, NB) as b:
                gelus(b, range(NCH), False)

        @block.tensor
        def _(pe):
            mm = nc.tensor.matmul
            pe.wait_ge(ld_mod, 32)
            pe.wait_ge(s_sil, 1)
            for k, col in ((0, 1), (1, 0)):
                last = mm(bank[0][:, k * NB:(k + 1) * NB], WMOD[:, col * P:(col + 1) * P], SIL[:, 3, :],
                          start=True, stop=True)
            last.then_inc(s_modp, 1)
            mm(bank[2][0:NB, :], SIL[:, 3, :], WMOD[:, 2 * P:6 * P], start=True, stop=True).then_inc(s_mod8p, 1)
            pe.wait_ge(s_const, 3)
            pe.wait_ge(s_modt, 1)

            def transposes(dst, src):
                for j in range(NJ):
                    last = nc.tensor.transpose(tok(dst, j), tok(src, j), IDENT[:])
                return last

            def gates_transpose(g):
                pe.wait_ge(s_w, g + 1)
                pe.wait_ge(s_gz, 5 if g == 0 else NB)
                nc.tensor.transpose(bank[7][:, 0:P], GT[:, 4, :, :].rearrange("p a e -> p (a e)"),
                                    IDENT[:]).then_inc(s_wt, 1)

            def transpose_first_norm(b):
                pe.wait_ge(s_xn1, b + 1)
                if b > 0:
                    pe.wait_ge(s_h1, b)
                transposes(bank[0], XN[:, b % G, :]).then_inc(s_xn1t, 1)

            def project(b):
                if b == 0:
                    pe.wait_ge(s_mod8, 1)
                    pe.wait_ge(s_bqv, 2)
                    pe.wait_ge(ld_qv, 48)
                pe.wait_ge(s_h1, b + 1)
                for k, done, read in ((0, s_q, s_qs), (1, s_v, s_vc)):
                    acc = bank[2 + 2 * k]
                    if b > 0:
                        pe.wait_ge(read, b)
                    mm(acc[:], ONESR[0:64, :], BQV[:, k:k + 1, :].to_broadcast([64, NJ, P]),
                       start=True, stop=False, skip_group_check=True)
                    for j in range(NJ):
                        last = mm(tok(acc, j), tok(HT[:, b % G, :], j), WQV[:, k, :], start=False,
                                  stop=(j == NJ - 1), skip_group_check=True)
                    last.then_inc(done, 1)

            def transpose_softmax(b):
                pe.wait_ge(s_p, b + 1)
                if b > 0:
                    pe.wait_ge(s_ptc, b)
                transposes(bank[3], PR[:, b % G, :]).then_inc(s_pt, 1)

            def contexts(b):
                pe.wait_ge(s_kx, b + 1)
                pe.wait_ge(s_vc, b + 1)
                if b > 0:
                    pe.wait_ge(s_ct, b)
                for j in range(NJ):
                    last = mm(bank[1][:, 0:P], tok(V[:, b % G, :], j), tok(EX[:, b % G, :], j), start=(j == 0),
                              stop=(j == NJ - 1))
                last.then_inc(s_ctx, 1)

            def context_wo(b):
                if b == 0:
                    pe.wait_ge(ld_small, 112)
                pe.wait_ge(s_ct, b + 1)
                if b > 0:
                    pe.wait_ge(s_ms, b)
                mm(bank[5][:, 0:P], CTX[:, b % G, :], WO[:], start=True, stop=True).then_inc(s_m, 1)

            def attend(b):
                pe.wait_ge(s_ms, b + 1)
                pe.wait_ge(s_ptc, b + 1)
                if b > 0:
                    pe.wait_ge(s_x1, b)
                for j in range(NJ):
                    last = mm(tok(bank[6], j), tok(HT[:, b % G, :], j), MS[:, b % G, :], start=True, stop=True)
                last.then_inc(s_att, 1)

            def transpose_third_norm(b):
                pe.wait_ge(s_xn3, b + 1)
                if b > 0:
                    pe.wait_ge(s_gz, b)
                if b == 5:
                    pe.wait_ge(s_wtc, 1)
                transposes(bank[7], XN[:, b % G, :]).then_inc(s_xn3t, 1)

            def logits(b):
                pe.wait_ge(s_xf, b + 1)
                mm(bank[7][:, 0:NJ * E], ONESR[0:1, :].bitcast(F32), BG[:].unsqueeze(1).to_broadcast([1, NJ, E]),
                   start=True, stop=False, skip_group_check=True)
                for j in range(NJ):
                    last = mm(bank[7][:, j * E:(j + 1) * E], tok(PR[:, b % G, :], j), WG[:], start=False,
                              stop=(j == NJ - 1), skip_group_check=True)
                last.then_inc(s_lg, 1)

            def first_product(b, n, first):
                done = b * NCH + n
                e, c = n // CH, n % CH
                if first and n == 0:
                    pe.wait_ge(s_xl, 1)
                if first and c == 0:
                    pe.wait_ge(s_wl, 2 * (e + 1))
                if not (first and n < RING):
                    pe.wait_ge(s_gelu, done - RING + 1)
                w = slice(e * 1024 + c * P, e * 1024 + (c + 1) * P)
                at = ds(b * TOK, TOK)
                mm(bank[n % RING][:], WH[:, w], XH[:, at], start=True, stop=False)
                mm(bank[n % RING][:], WH[:, w], XL[:, at], start=False, stop=False)
                mm(bank[n % RING][:], WL[:, w], XH[:, at], start=False, stop=True).then_inc(s_pre, 1)

            def second_product(b, n, first):
                done = b * NCH + n
                e, c, slot = n // CH, n % CH, n % RING
                y = bank[4 + e % 2]
                if c == 0 and not (first and e < 2):
                    pe.wait_ge(s_yread, b * E + e - 1)
                w = slice(e * 1024 + 512 + c * P, e * 1024 + 512 + (c + 1) * P)
                pe.wait_ge(s_gelu, done + 1)
                mm(y[:], WH[:, w], HH[:, slot, :], start=(c == 0), stop=False)
                mm(y[:], WL[:, w], HH[:, slot, :], start=False, stop=False)
                pe.wait_ge(s_hl, done + 1)
                mm(y[:], WH[:, w], HL[:, slot, :], start=False, stop=(c == CH - 1)).then_inc(s_used, 1)

            def output_transposes(b):
                pe.wait_ge(s_yt, b + 1)
                transposes(bank[6], YT).then_inc(s_ytt, 1)

            def experts(b, chunks, first):
                for n in chunks:
                    first_product(b, n, first)
                    if n >= LAG:
                        second_product(b, n - LAG, first)
                    elif not first:
                        second_product(b - 1, n - LAG + NCH, False)
                    if n == 7 and not first:
                        output_transposes(b - 1)
                    if first and n == LATE + 17:
                        gates_transpose(NG - 1)

            stages = {4: transpose_first_norm, 8: project, 11: transpose_softmax, 12: contexts, 13: context_wo,
                      16: attend, 25: transpose_third_norm, 27: logits}
            for t in range(STEPS):
                at_step(t, stages)
                if t == GATES_STEP + 6:
                    gates_transpose(0)
                experts(0, early_chunks(t), True)
            experts(0, range(LATE, NCH), True)
            pe.wait_ge(s_xl, NB)
            with pe.Fori(1, NB) as b:
                experts(b, range(NCH), False)
            for n in range(NCH - LAG, NCH):
                second_product(NB - 1, n, False)
            output_transposes(NB - 1)

        @block.vector
        def _(dve):
            v = nc.vector
            v.memset(BRAW[:], 0.0).then_inc(s_zero, 1)
            for e in range(E):
                last = v.memset(RANK[:, e:e + 1], float(E - e))
            last.then_inc(s_dset, 1)
            dve.wait_ge(s_es, 1)
            dve.wait_ge(ld_mod, 32)
            v.tensor_scalar(SIL[:, 1, :], SIL[:, 0, :], 1.0, None, ALU.add).then_inc(s_dset, 1)
            dve.wait_ge(s_dset, 2)
            v.reciprocal(SIL[:, 2, :], SIL[:, 1, :]).then_inc(s_dset, 1)
            dve.wait_ge(s_dset, 3)
            v.tensor_tensor(SIL[:, 3, :], CT[:], SIL[:, 2, :], ALU.mult).then_inc(s_sil, 1)

            def stats(k, b, src):
                for j in range(NJ):
                    last = v.bn_stats(ST[:, k, b * NJ + j, :], tok(src, j))
                last.then_inc(s_st[k], 1)
                dve.wait_ge(s_st[k], b + 1)
                for j in range(NJ):
                    last = v.bn_aggr(MV[:, k, b * NJ + j, :], ST[:, k, b * NJ + j, :])
                last.then_inc(s_mv[k], 1)

            def shift(k, b):
                at = slice(b * NJ, (b + 1) * NJ)
                dve.wait_ge(s_rstd[k], b + 1)
                v.scalar_tensor_tensor(out=NMR[:, k, at], in0=MV[:, k, at, 0], scalar=-1.0, in1=RSTD[:, k, at],
                                       op0=ALU.mult, op1=ALU.mult).then_inc(s_nmr[k], 1)

            def modulation_columns():
                dve.wait_ge(s_modp, 1)
                v.tensor_scalar(MODT[:, 0, :], bank[0][:, 0:NB], 1.0, None, ALU.add)
                v.tensor_copy(MODT[:, 1, :], bank[0][:, NB:2 * NB]).then_inc(s_modt, 1)

            def bias_split():
                dve.wait_ge(ld_qv, 48)
                dve.wait_ge(s_const, 1)
                v.tensor_copy(ONESR[:], ONES[:]).then_inc(s_bqv, 1)
                v.tensor_copy(BQV[:], BRAW[:]).then_inc(s_dset, 1)
                dve.wait_ge(s_dset, 4)
                v.tensor_tensor(BQV[32:64, :, :], BRAW[32:64, :, :], BQV[32:64, :, :].bitcast(F32),
                                ALU.subtract).then_inc(s_bqv, 1)

            def modulation_rows():
                dve.wait_ge(s_mod8p, 1)
                v.tensor_copy(MOD8[:, 0:4, :], bank[2][0:NB, :].rearrange("p (r n) -> p r n", r=4)).then_inc(s_dset, 1)
                dve.wait_ge(s_dset, 5)
                g8 = MOD8[:, 0:4:3, :]
                v.scalar_tensor_tensor(out=MAG8[:, 0, :, :], in0=g8, scalar=-1.0, in1=g8, op0=ALU.mult,
                                       op1=ALU.max).then_inc(s_dset, 1)
                v.tensor_scalar(MAG8[:, 1, :, :], g8, 0.0, 2.0, ALU.is_ge, ALU.mult).then_inc(s_dset, 1)
                v.tensor_scalar(MOD8[:, 2, :], MOD8[:, 2, :], 1.0, None, ALU.add).then_inc(s_dset, 1)
                dve.wait_ge(s_dset, 8)
                v.tensor_scalar(MAG8[:, 2, :, :], MAG8[:, 0, :, :], 0.25, None, ALU.max).then_inc(s_dset, 1)
                dve.wait_ge(s_dset, 9)
                v.scalar_tensor_tensor(out=g8, in0=MAG8[:, 1, :, :], scalar=1.0, in1=MAG8[:, 2, :, :],
                                       op0=ALU.subtract, op1=ALU.mult).then_inc(s_dset, 1)
                dve.wait_ge(s_dset, 10)
                dve.wait_ge(ld_small, 112)
                v.scalar_tensor_tensor(out=MOD8[:, 4, :], in0=MOD8[:, 0, :], scalar=1.0 / HEADS, in1=BO[:],
                                       op0=ALU.mult, op1=ALU.mult).then_inc(s_mod8, 1)

            z, ez, first_hot, eq, rest = (GT[:, k, :, :] for k in range(5))
            pr, second_hot, w = ez, eq, rest
            top, total, inv, best, rank1, second, rank2, scale = (GS[:, k, :] for k in range(8))
            linked = [0]

            def wide(t):
                return t.unsqueeze(2).to_broadcast([P, G * NJ, E])

            def link(ins):
                linked[0] += 1
                ins.then_inc(s_gate, 1)
                dve.wait_ge(s_gate, linked[0])

            def gates_shift(b):
                at = slice(b % G * NJ, (b % G + 1) * NJ)
                dve.wait_ge(s_lg, b + 1)
                part = bank[7][:, 0:NJ * E].rearrange("p (a e) -> p a e", e=E)
                v.tensor_reduce(top[:, at], part, AX.X, ALU.max).then_inc(s_top, 1)
                dve.wait_ge(s_top, b + 1)
                if b >= G:
                    dve.wait_ge(s_gez, 1)
                v.tensor_tensor(z[:, at, :], part, top[:, at].unsqueeze(2).to_broadcast([P, NJ, E]),
                                ALU.subtract).then_inc(s_gz, 1)

            def gates_steps(g, ks):
                for k in ks:
                    if k == 0:
                        dve.wait_ge(s_gez, g + 1)
                        link(v.tensor_reduce(total, ez, AX.X, ALU.add))
                    elif k == 1:
                        link(v.reciprocal(inv, total))
                    elif k == 2:
                        link(v.tensor_tensor(pr, ez, wide(inv), ALU.mult))
                    elif k == 3:
                        link(v.tensor_reduce(best, pr, AX.X, ALU.max))
                    elif k == 4:
                        link(v.tensor_tensor(eq, pr, wide(best), ALU.is_equal))
                    elif k in (5, 11):
                        link(v.tensor_tensor(eq, eq, RANK[:].unsqueeze(1).to_broadcast([P, G * NJ, E]), ALU.mult))
                    elif k == 6:
                        link(v.tensor_reduce(rank1, eq, AX.X, ALU.max))
                    elif k == 7:
                        link(v.tensor_tensor(first_hot, eq, wide(rank1), ALU.is_equal))
                    elif k == 8:
                        if g > 0:
                            dve.wait_ge(s_wt, g)
                        link(v.scalar_tensor_tensor(out=rest, in0=first_hot, scalar=-2.0, in1=pr, op0=ALU.mult,
                                                    op1=ALU.add))
                    elif k == 9:
                        link(v.tensor_reduce(second, rest, AX.X, ALU.max))
                    elif k == 10:
                        link(v.tensor_tensor(eq, rest, wide(second), ALU.is_equal))
                    elif k == 12:
                        link(v.tensor_reduce(rank2, eq, AX.X, ALU.max))
                    elif k == 13:
                        link(v.tensor_tensor(second_hot, eq, wide(rank2), ALU.is_equal))
                    elif k == 14:
                        link(v.tensor_tensor(first_hot, first_hot, second_hot, ALU.add))
                    elif k == 15:
                        link(v.tensor_tensor(scale, best, second, ALU.add))
                    elif k == 16:
                        link(v.tensor_scalar(scale, scale, EPS_TOPK, None, ALU.add))
                    elif k == 17:
                        link(v.reciprocal(scale, scale))
                    elif k == 18:
                        link(v.tensor_tensor(w, pr, first_hot, ALU.mult))
                    elif k == 19:
                        v.tensor_tensor(w, w, wide(scale), ALU.mult).then_inc(s_w, 1)

            def first_stats(b):
                dve.wait_ge(ld_x[b], 16)
                stats(0, b, X[:, xs(b)])

            def first_shift(b):
                shift(0, b)

            def head_maxima(b):
                q = bank[2][:].rearrange(heads, k=DH)
                dve.wait_ge(s_q, b + 1)
                v.tensor_reduce(SM[:, b % 2, 0, :], q, AX.X, ALU.max).then_inc(s_mx, 1)
                dve.wait_ge(s_mx, b + 1)
                v.tensor_tensor(EX[:, b % G, :].rearrange(heads, k=DH), q,
                                SM[:, b % 2, 0, :].unsqueeze(2).to_broadcast([P, HEADS * NJ, DH]),
                                ALU.subtract).then_inc(s_qs, 1)

            def head_softmax(b):
                ex = EX[:, b % G, :].rearrange(heads, k=DH)
                dve.wait_ge(s_e, b + 1)
                v.tensor_reduce(SM[:, b % 2, 1, :], ex, AX.X, ALU.add).then_inc(s_sm, 1)
                dve.wait_ge(s_sm, b + 1)
                if b >= 2:
                    dve.wait_ge(s_p, b - 1)
                v.reciprocal(SM[:, b % 2, 2, :], SM[:, b % 2, 1, :]).then_inc(s_rc, 1)

            def mask_context(b):
                dve.wait_ge(s_ctx, b + 1)
                v.tensor_tensor(CTX[:, b % G, :], bank[1][:, 0:P], HMASK[:].rearrange("p m k -> p (m k)"), ALU.mult)
                dve.wait_ge(s_ptc, b + 1)
                v.reciprocal(RDEN[:, 1, b % G:b % G + 1], RDEN[:, 0, b % G:b % G + 1]).then_inc(s_ct, 1)

            def scale_context(b):
                if b == 0:
                    dve.wait_ge(ld_rows, 16)
                dve.wait_ge(s_m, b + 1)
                v.scalar_tensor_tensor(out=MS[:, b % G, :], in0=bank[5][:, 0:P], scalar=RDEN[:, 1, b % G:b % G + 1],
                                       in1=ROWS[:, b, 0, :], op0=ALU.mult, op1=ALU.mult).then_inc(s_msa, 1)
                dve.wait_ge(s_msa, b + 1)
                v.tensor_tensor(MS[:, b % G, :], MS[:, b % G, :], ROWS[:, b, 4, :], ALU.add).then_inc(s_ms, 1)

            def add_attention(b):
                dve.wait_ge(s_att, b + 1)
                v.tensor_tensor(X[:, xs(b)], bank[6][:], X[:, xs(b)], ALU.add).then_inc(s_x1, 1)
                dve.wait_ge(s_x1, b + 1)
                stats(1, b, X[:, xs(b)])

            def center(b):
                dve.wait_ge(s_mv[1], b + 1)
                for j in range(NJ):
                    v.scalar_tensor_tensor(out=tok(V[:, b % G, :], j), in0=tok(X[:, xs(b)], j),
                                           scalar=MV[:, 1, b * NJ + j, 0:1], in1=ROWS[:, b, 2, :],
                                           op0=ALU.subtract, op1=ALU.mult).then_inc(s_cen, 1)

            def second_norm(b):
                dve.wait_ge(s_rstd[1], b + 1)
                dve.wait_ge(s_cen, (b + 1) * NJ)
                for j in range(NJ):
                    a = b * NJ + j
                    last = v.scalar_tensor_tensor(out=tok(V[:, b % G, :], j), in0=tok(V[:, b % G, :], j),
                                                  scalar=RSTD[:, 1, a:a + 1], in1=ROWS[:, b, 1, :],
                                                  op0=ALU.mult, op1=ALU.add)
                last.then_inc(s_h2, 1)
                dve.wait_ge(s_h2, b + 1)
                stats(2, b, V[:, b % G, :])

            def third_shift(b):
                shift(2, b)


            def lo(b, n, first):
                slot = n % RING
                done = b * NCH + n
                dve.wait_ge(s_gelu, done + 1)
                if not (first and n < RING):
                    dve.wait_ge(s_used, done - RING + 1)
                v.tensor_tensor(HL[:, slot, :], HF[:, slot, :], HH[:, slot, :].bitcast(F32),
                                ALU.subtract).then_inc(s_hl, 1)

            def gated(b, e, first=False):
                done = b * E + e
                dve.wait_ge(s_used, done * CH + CH)
                dve.wait_ge(ld_wb[e], (b + 1) * 16)
                y = bank[4 + e % 2][:]
                if first and e in (0, 1, E - 1):
                    dve.wait_ge(s_xn3t, (G + e + 1) if e < 2 else NB)
                v.scalar_tensor_tensor(out=ACC if e == 0 else YW, in0=y, scalar=B2[:, e:e + 1], in1=WB[:, e, :],
                                       op0=ALU.add, op1=ALU.mult).then_inc(s_yread, 1)
                if e == 0:
                    return
                dve.wait_ge(s_yread, done + 1)
                if e > 1:
                    dve.wait_ge(s_acc, b * (E - 2) + e - 1)
                if e < E - 1:
                    v.tensor_tensor(ACC, ACC, YW, ALU.add).then_inc(s_acc, 1)
                else:
                    v.tensor_tensor(YT, ACC, YW, ALU.add).then_inc(s_yt, 1)

            def result(b):
                dve.wait_ge(s_ytt, b + 1)
                v.tensor_tensor(OT.rearrange("p (j d) -> p j d", j=NJ), bank[6][:].rearrange("p (j d) -> p j d", j=NJ),
                                ROWS[:, ds(b, 1), 3, :].to_broadcast([P, NJ, P]), ALU.mult).then_inc(s_o1, 1)
                dve.wait_ge(s_o1, b + 1)
                xr = X[:, ds(b * TOK, TOK)]
                v.tensor_tensor(xr, xr, OT, ALU.add).then_inc(s_res2, 1)

            def experts(b, chunks, first):
                for n in chunks:
                    lo(b, n, first)
                    if n % CH == 2 and n > CH:
                        gated(b, n // CH - 1, first)
                    if n == 2 and not first:
                        gated(b - 1, E - 1)
                    if n == 11 and not first:
                        result(b - 1)
                    if first and n >= GATES_CHUNK and n % CH != 2:
                        k = 2 * (n - GATES_CHUNK - (n + 1) // CH + (GATES_CHUNK + 1) // CH)
                        gates_steps(NG - 1, range(min(k, GATES_CHAIN), min(k + 2, GATES_CHAIN)))

            stages = {1: first_shift, 7: head_maxima, 9: head_softmax, 12: mask_context, 14: scale_context,
                      17: add_attention, 18: center, 19: second_norm, 21: third_shift, 27: gates_shift}
            first_stats(0)
            for t in range(STEPS):
                at_step(t, stages)
                for b in first_statistics(t):
                    first_stats(b)
                if t == 2:
                    modulation_columns()
                if t == 3:
                    bias_split()
                if t == 4:
                    modulation_rows()
                if t > GATES_STEP:
                    k = (t - GATES_STEP - 1) * GATES_PER_STEP
                    gates_steps(0, range(min(k, GATES_CHAIN), min(k + GATES_PER_STEP, GATES_CHAIN)))
                experts(0, early_chunks(t), True)
            experts(0, range(LATE, NCH), True)
            dve.wait_ge(s_res, NB)
            with dve.Fori(1, NB) as b:
                experts(b, range(NCH), False)
            gated(NB - 1, E - 1)
            result(NB - 1)


def kernel(**inputs):
    import numpy as _np
    import concourse.bacc as _bacc
    from concourse.bass_utils import run_bass_kernel_spmd as _run

    a = {k: _np.asarray(v) for k, v in inputs.items()}
    d, e, f = P, E, CH * P
    w1 = a["L0_ffn_W1"].transpose(2, 0, 1)
    w2 = a["L0_ffn_W2"].transpose(0, 2, 1).reshape(e, CH, P, d).transpose(2, 0, 1, 3).reshape(P, e, CH * d)
    arrays = {
        "x": a["L0_attn_x"],
        "wqv": _np.stack([a["L0_attn_Wq"], a["L0_attn_Wv"]], axis=1), "wo": a["L0_attn_Wo"],
        "bqv": _np.stack([a["L0_attn_bq"], a["L0_attn_bv"]])[None], "bo": a["L0_attn_bo"].reshape(1, d),
        "gb": _np.stack([a["L0_ffn_gamma"], a["L0_ffn_beta"]], axis=1),
        "wg": a["L0_ffn_Wg"].T, "bg": a["L0_ffn_bg"].reshape(1, e),
        "w12": _np.stack([w1, w2], axis=2).reshape(P, 2 * e * f),
        "b1": a["L0_ffn_b1"].reshape(e * CH, P).T, "b2": a["L0_ffn_b2"].T,
        "c_t": a["L0_c"].T, "wmod": a["L0_wmod"],
    }
    arrays = {k: _np.ascontiguousarray(v) for k, v in arrays.items()}
    nc = _bacc.Bacc("TRN2", target_bir_lowering=False, num_devices=1)
    args = {k: nc.dram_tensor(k, v.shape, F32, kind="ExternalInput").ap() for k, v in arrays.items()}
    mod_dram = nc.dram_tensor("mod_dram", (NB, 5, P), F32).ap()
    w_dram = nc.dram_tensor("w_dram", (NB, NJ, E, P), F32).ap()
    out = nc.dram_tensor("out", (NB, TOK, P), F32, kind="ExternalOutput").ap()
    adaln_block(nc, mod_dram=mod_dram, w_dram=w_dram, out=out, **args)
    r = _run(nc, [arrays], core_ids=[0])
    return r.results[0]["out"]
```
